# Optimizing a Trainium2 kernel written in Bass

```python
import numpy as np
import jax
import jax.numpy as jnp

def _softmax(x, axis=-1):
    return jax.nn.softmax(x, axis=axis)

def _gelu(x):
    return jax.nn.gelu(x, approximate=True)

def _silu(x):
    return jax.nn.silu(x)

def _sigmoid(x):
    return jax.nn.sigmoid(x)

def _layernorm(x, axis=-1, eps=1e-05):
    m = jnp.mean(x, axis=axis, keepdims=True)
    v = jnp.var(x, axis=axis, keepdims=True)
    return (x - m) / jnp.sqrt(v + eps)

def _scatter_add(tgt, idx, src, axis=0):
    return tgt.at[idx].add(src)

def _segment_sum(src, seg, n):
    return jax.ops.segment_sum(src, seg, n)
kernel_name = 'mk_seq_preln_d1_jaxref_r8_44b17c'

def setup_inputs(seed: int=0):
    np.random.seed(seed)
    _w = jnp.asarray

    def _L0_attn_setup():
        import jax, jax.numpy as jnp
        import numpy as np
        B, S, D, H = (2, 256, 128, 16)
        HD = D // H
        key = jax.random.key(seed)
        ks = jax.random.split(key, 5)
        scale = 1.0 / np.sqrt(D)
        x = jax.random.normal(ks[0], (B, S, D), dtype=jnp.float32)
        W_Q = jax.random.uniform(ks[1], (D, D), jnp.float32, -scale, scale)
        W_K = jax.random.uniform(ks[2], (D, D), jnp.float32, -scale, scale)
        W_V = jax.random.uniform(ks[3], (D, D), jnp.float32, -scale, scale)
        W_O = jax.random.uniform(ks[4], (D, D), jnp.float32, -scale, scale)
        return {'x': x, 'W_Q': W_Q, 'W_K': W_K, 'W_V': W_V, 'W_O': W_O}
    _L0_attn_in = _L0_attn_setup()

    def _L0_ffn_setup():
        import jax, jax.numpy as jnp
        import numpy as np
        E = 8
        K = 2
        key = jax.random.key(seed)
        ks = jax.random.split(key, 6)
        B, S, D, F = (4, 256, 128, 512)
        s_d = 1.0 / np.sqrt(D).astype(np.float32)
        s_f = 1.0 / np.sqrt(F).astype(np.float32)
        return {'x': jax.random.normal(ks[0], (B, S, D), jnp.float32), 'ln_w': jnp.ones((D,), jnp.float32), 'Wg': jax.random.normal(ks[1], (D, E), jnp.float32) * s_d, 'bg': jnp.zeros((E,), jnp.float32), 'W1a': jax.random.normal(ks[2], (E, D, F), jnp.float32) * s_d, 'b1a': jnp.zeros((E, F), jnp.float32), 'W1b': jax.random.normal(ks[3], (E, D, F), jnp.float32) * s_d, 'b1b': jnp.zeros((E, F), jnp.float32), 'W2': jax.random.normal(ks[4], (E, F, D), jnp.float32) * s_f, 'b2': jnp.zeros((E, D), jnp.float32)}
    _L0_ffn_in = _L0_ffn_setup()
    _d = {'L0_attn_x': _L0_attn_in['x'], 'L0_attn_W_Q': _L0_attn_in['W_Q'], 'L0_attn_W_K': _L0_attn_in['W_K'], 'L0_attn_W_V': _L0_attn_in['W_V'], 'L0_attn_W_O': _L0_attn_in['W_O'], 'L0_ffn_ln_w': _L0_ffn_in['ln_w'], 'L0_ffn_Wg': _L0_ffn_in['Wg'], 'L0_ffn_bg': _L0_ffn_in['bg'], 'L0_ffn_W1a': _L0_ffn_in['W1a'], 'L0_ffn_b1a': _L0_ffn_in['b1a'], 'L0_ffn_W1b': _L0_ffn_in['W1b'], 'L0_ffn_b1b': _L0_ffn_in['b1b'], 'L0_ffn_W2': _L0_ffn_in['W2'], 'L0_ffn_b2': _L0_ffn_in['b2']}
    _x0 = _d['L0_attn_x']
    _d['L0_attn_x'] = jax.random.normal(jax.random.fold_in(jax.random.key(seed), 1), (32, 256, 128), dtype=_x0.dtype)
    del _x0
    return _d

def reference(L0_attn_x, L0_attn_W_Q, L0_attn_W_K, L0_attn_W_V, L0_attn_W_O, L0_ffn_ln_w, L0_ffn_Wg, L0_ffn_bg, L0_ffn_W1a, L0_ffn_b1a, L0_ffn_W1b, L0_ffn_b1b, L0_ffn_W2, L0_ffn_b2):

    def _L0_attn_ref(x, W_Q, W_K, W_V, W_O):
        import jax, jax.numpy as jnp
        import numpy as np
        B, S, D, H = (2, 256, 128, 16)
        HD = D // H
        b, s, d = x.shape
        Q = (x @ W_Q.T).reshape(b, s, H, HD).transpose(0, 2, 1, 3)
        K = (x @ W_K.T).reshape(b, s, H, HD).transpose(0, 2, 1, 3)
        V = (x @ W_V.T).reshape(b, s, H, HD).transpose(0, 2, 1, 3)
        attn = jnp.einsum('bhqd,bhkd->bhqk', Q, K) / jnp.sqrt(jnp.float32(HD))
        slopes = 1.0 / (2.0 ** 8) ** ((jnp.arange(H, dtype=jnp.float32) + 1) / H)
        pos = jnp.arange(s)
        rel = jnp.minimum(pos[None, :] - pos[:, None], 0).astype(jnp.float32)
        bias = slopes[:, None, None] * rel[None, :, :]
        causal = pos[None, :] <= pos[:, None]
        attn = jnp.where(causal[None, None], attn + bias[None], -jnp.inf)
        attn = jax.nn.softmax(attn, axis=-1)
        out = jnp.einsum('bhqk,bhkd->bhqd', attn, V)
        out = out.transpose(0, 2, 1, 3).reshape(b, s, d)
        return out @ W_O.T

    def _L0_ffn_ref(x, ln_w, Wg, bg, W1a, b1a, W1b, b1b, W2, b2):
        import jax, jax.numpy as jnp
        import numpy as np
        E = 8
        K = 2
        B, S, D = x.shape
        eps = jnp.finfo(x.dtype).eps
        xn = x * jax.lax.rsqrt(jnp.mean(x * x, axis=-1, keepdims=True) + eps) * ln_w
        logits = xn @ Wg + bg
        vals, idx = jax.lax.top_k(logits, K)
        topk_w = jax.nn.softmax(vals, axis=-1)
        we = jnp.sum(jax.nn.one_hot(idx, E, dtype=x.dtype) * topk_w[..., None], axis=-2)
        T = B * S
        xf = xn.reshape(T, D)
        wef = we.reshape(T, E).T

        def step(acc, params):
            W1a_e, b1a_e, W1b_e, b1b_e, W2_e, b2_e, w_e = params
            a = xf @ W1a_e + b1a_e
            b = xf @ W1b_e + b1b_e
            y = jax.nn.silu(a) * b @ W2_e + b2_e
            return (acc + w_e[:, None] * y, None)
        out0 = jnp.zeros_like(xf)
        out, _ = jax.lax.scan(step, out0, (W1a, b1a, W1b, b1b, W2, b2, wef))
        return out.reshape(B, S, D)
    x = L0_attn_x
    x = x + _L0_attn_ref(_layernorm(x, axis=-1), L0_attn_W_Q, L0_attn_W_K, L0_attn_W_V, L0_attn_W_O)
    x = x + _L0_ffn_ref(_layernorm(x, axis=-1), L0_ffn_ln_w, L0_ffn_Wg, L0_ffn_bg, L0_ffn_W1a, L0_ffn_b1a, L0_ffn_W1b, L0_ffn_b1b, L0_ffn_W2, L0_ffn_b2)
    return x

_drawn_inputs = setup_inputs


def setup_inputs(seed=0):
    import zlib

    import numpy as np

    out = dict(_drawn_inputs(seed))
    spreads = {'L0_ffn_ln_w': (1.0, 0.2),
     'L0_ffn_bg': (0.0, 0.1),
     'L0_ffn_b1a': (0.0, 0.1),
     'L0_ffn_b1b': (0.0, 0.1),
     'L0_ffn_b2': (0.0, 0.1)}
    factors = {}
    for name, (base, spread) in spreads.items():
        noise = np.random.default_rng([zlib.crc32(name.encode()), seed]).standard_normal(out[name].shape)
        drawn = base * np.exp(spread * noise) if base else spread * noise
        out[name] = jnp.asarray(drawn.astype(out[name].dtype))
    for name, factor in factors.items():
        out[name] = (out[name] * factor).astype(out[name].dtype)
    return out
```

```python
import concourse.bass as bass
from concourse import mybir
from contextlib import ExitStack


def build_program(nc, x_in, wq_in, wk_in, wv_in, wo_in, const_f32, const_bf16, ln_w_in, wg_in, bg_in, w1a_in, b1a_in,
                  w1b_in, b1b_in, w2_in, b2_in, route_f32, route_bf16, out):
    fp32 = mybir.dt.float32
    fp32r = mybir.dt.float32r
    bf16 = mybir.dt.bfloat16
    i32, u32 = mybir.dt.int32, mybir.dt.uint32
    ALU = mybir.AluOpType
    ACT = mybir.ActivationFunctionType
    AX = mybir.AxisListType

    P = 128
    NB, S, D = x_in.shape
    H, HD = 16, 8
    NT = S // P
    NC, NG = 4, 4
    TILES = NB * NT
    EPS = 1e-5
    RMS_EPS = 2.0 ** -23
    E, _, F = w1a_in.shape
    FC = F // P
    SLOT_TILES = 2 * TILES + E
    QK_SCALE = float(HD) ** -0.5

    ctx = ExitStack()
    with ctx:
        def sb(name, shape, dt):
            return ctx.enter_context(nc.sbuf_tensor(name, shape, dt))

        def sem(name):
            return ctx.enter_context(nc.semaphore(name))

        xs = sb("xs", [P, TILES, D], fp32)
        cf = sb("cf", [P, 3 + P], fp32)
        minus_half, lo_rows_q, lo_rows_k = cf[:, 0:1], cf[:, 1:2], cf[:, 2:3]
        ident = cf[:, 3:3 + P]
        mv_all = sb("mv_all", [P, TILES, 2], fp32)
        xs_dram = nc.dram_tensor("expert_inputs", [SLOT_TILES * P, D], fp32, kind="Internal").ap()
        ys_dram = nc.dram_tensor("expert_outputs", [SLOT_TILES * P, D], fp32, kind="Internal").ap()
        zero_filled = sem("zero_filled")

        def wait(eng, semaphore, value):
            if not isinstance(value, int) or value > 0:
                eng.wait_ge(semaphore, value)

        with ExitStack() as part_a:
            def sba(name, shape, dt):
                return part_a.enter_context(nc.sbuf_tensor(name, shape, dt))

            wq = sba("wq", [P, NC, P], fp32)
            wk = sba("wk", [P, NC, P], fp32)
            wv = sba("wv", [P, D], fp32)
            wo = sba("wo", [P, D], fp32)
            cb = sba("cb", [P, P + 8 * P + S + 2 * NC * P], bf16)
            causalT = cb[:, 5 * P:9 * P]
            ident_bf = cb[:, 0:P]
            causal = cb[:, P:5 * P]
            pos_rows = cb[:, 9 * P:9 * P + S]
            const_q = cb[:, 9 * P + S:9 * P + S + NC * P].rearrange("p (c m) -> p c m", c=NC)
            const_k = cb[:, 9 * P + S + NC * P:].rearrange("p (c m) -> p c m", c=NC)

            stats = sba("stats", [P, NT, 6], fp32)
            mean_var = sba("mean_var", [P, NT, 2], fp32)
            var_eps = sba("var_eps", [P, NT], fp32)
            rstd = sba("rstd", [P, NT], fp32)
            xn = sba("xn", [P, NT, D], fp32)
            xnT = sba("xnT", [P, S], fp32)
            hi = sba("hi", [P, 2, 2, S], fp32r)
            qs = sba("qs", [P, NC, S], fp32r)
            ks = sba("ks", [P, 2, NC, S], fp32r)
            qm = [sba(f"qm{i}", [P, NC, NG, S], fp32r) for i in range(2)]
            km = sba("km", [P, NC, NG, S], fp32r)
            va = sba("va", [P, 2, NT, H, 32], fp32)
            negmax = sba("negmax", [P, NT, NG, NC], fp32)
            maxT = sba("maxT", [H, 2, S], fp32r)
            pk0 = sba("pk0", [P, 2, NG, S], fp32)
            pk1 = sba("pk1", [P, H, P], fp32)
            oT = sba("oT", [P, NC, S], fp32)
            rden = sba("rden", [P, NT, H], fp32)
            on = sba("on", [P, NT, H, HD], fp32)
            onT = sba("onT", [P, S], fp32)

            zeros = sba("zeros", [P, SLOT_TILES * D // 16], fp32)
            mv1 = sba("mv1", [P, NT, 2], fp32)
            stats1 = sba("stats1", [P, NT, 6], fp32)
            bn1 = sem("bn1")
            mv1_ready = sem("mv1_ready")
            zeros_ready = sem("zeros_ready")
            turn_a = sem("turn_a")
            turn_p = sem("turn_p")
            s1 = part_a.enter_context(nc.psum_tensor("s1", [P, 2, 512], fp32))
            s2 = part_a.enter_context(nc.psum_tensor("s2", [P, 2, 512], fp32))
            X = [part_a.enter_context(nc.psum_tensor(f"x{i}", [P, 512], fp32)) for i in range(4)]

            x_loaded = sem("x_loaded")
            w_loaded = sem("w_loaded")
            wq_scaled = sem("wq_scaled")
            zeroed = sem("zeroed")
            bn = sem("bn")
            stats_ready = sem("stats_ready")
            var_ready = sem("var_ready")
            rstd_ready = sem("rstd_ready")
            xn_ready = sem("xn_ready")
            xnT_ps = sem("xnT_ps")
            xnT_ready = sem("xnT_ready")
            proj_ps = sem("proj_ps")
            hi_ready = sem("hi_ready")
            stack_ready = sem("stack_ready")
            km_ready = sem("km_ready")
            qm_ready = sem("qm_ready")
            v_ps = sem("v_ps")
            v_ready = sem("v_ready")
            s1_ps = sem("s1_ps")
            max_ready = sem("max_ready")
            maxT_ps = sem("maxT_ps")
            max_hi = sem("max_hi")
            maxT_ready = sem("maxT_ready")
            max_placed = sem("max_placed")
            s2_ps = sem("s2_ps")
            exp_ready = sem("exp_ready")
            pv_ps = sem("pv_ps")
            oT_ready = sem("oT_ready")
            oq_ps = sem("oq_ps")
            rden_ready = sem("rden_ready")
            on_ready = sem("on_ready")
            onT_ps = sem("onT_ps")
            onT_ready = sem("onT_ready")
            y_ps = sem("y_ps")
            x1_ready = sem("x1_ready")
            stored = sem("stored")

            def schedule(eng, iteration):
                iteration(-1, project=True, attend=False, finish=False)
                iteration(0, project=True, attend=True, finish=False)
                with eng.Fori(1, NB - 3, 2) as i:
                    iteration(i, project=True, attend=True, finish=True)
                    iteration(i + 1, project=True, attend=True, finish=True, even=True)
                iteration(NB - 3, project=True, attend=True, finish=True)
                iteration(NB - 2, project=True, attend=True, finish=True)
                iteration(NB - 1, project=False, attend=True, finish=True)
                iteration(NB, project=False, attend=False, finish=True)

            def parity(i, even):
                return i % 2 if isinstance(i, int) else (0 if even else 1)

            block = part_a.enter_context(nc.Block())

            @block.sync
            def _(sp):
                sp.dma_start(cf[:, :], const_f32).then_inc(w_loaded, 16)
                sp.dma_start(cb[:, :], const_bf16).then_inc(w_loaded, 16)
                sp.dma_start(wq[:, :, :], wq_in).then_inc(w_loaded, 16)
                sp.dma_start(wk[:, :, :], wk_in).then_inc(w_loaded, 16)
                sp.dma_start(wv[:, :], wv_in).then_inc(w_loaded, 16)
                sp.dma_start(wo[:, :], wo_in).then_inc(w_loaded, 16)
                for b in range(NB):
                    sp.dma_start(xs[:, NT * b:NT * b + NT, :], x_in[b].rearrange("(t p) d -> p t d", p=P)).then_inc(x_loaded, 16)

                sp.wait_ge(zeros_ready, 1)
                fill = xs_dram.rearrange("(p r) d -> p (r d)", p=P)
                width = SLOT_TILES * D // 16
                for n in range(16):
                    sp.dma_start(fill[:, n * width:(n + 1) * width], zeros[:, :]).then_inc(zero_filled, 16)

                def iteration(i, project, attend, finish, even=False):
                    if attend:
                        sp.wait_ge(qm_ready, i + 1)
                        sp.wait_ge(maxT_ready, i + 1)
                        for g in range(NG):
                            for part in range(2):
                                row = 32 * g + 28 + part
                                sp.dma_start(qm[parity(i, even)][row:row + 1, :, g, :].bitcast(fp32),
                                             maxT[NC * g:NC * g + NC, part, :].bitcast(fp32)).then_inc(max_placed, 16)
                schedule(sp, iteration)
                sp.wait_ge(zero_filled, 256)

            @block.gpsimd
            def _(pool):
                def masked_queries(n, par, done):
                    pool.wait_ge(stack_ready, 4 * n + 4)
                    wait(pool, s2_ps, 6 * (n - 1))
                    pool.wait_ge(rstd_ready, n + 1)
                    pool.sem_inc(turn_p, 1)
                    for g in range(NG):
                        last = nc.gpsimd.tensor_scalar(qm[par][32 * g:32 * g + 32, :, g, :],
                                                       qs[32 * g:32 * g + 32, :, :].bitcast(fp32), 1.0, 0.0,
                                                       ALU.mult, ALU.add)
                    last.then_inc(qm_ready, 1)

                def zero(buf):
                    return nc.gpsimd.memset(buf.bitcast(fp32), 0.0)

                nc.gpsimd.memset(zeros[:, :], 0.0).then_inc(zeros_ready, 1)
                zero(qm[0][:, :, :, :])
                zero(qm[1][:, :, :, :])
                nc.gpsimd.memset(va[:, :, :, :, :].rearrange("p a t h e -> p (a t h e)"), 0.0).then_inc(zeroed, 1)
                pool.wait_ge(zeroed, 1)
                nc.gpsimd.memset(va[:, :, :, :, HD:HD + 1], 1.0).then_inc(zeroed, 1)

                def inverse_deviation(n):
                    pool.wait_ge(stats_ready, n + 1)
                    wait(pool, qm_ready, n)
                    pool.sem_inc(turn_p, 1)
                    nc.gpsimd.tensor_scalar(var_eps[:, :], mean_var[:, :, 1], 1.0, EPS, ALU.mult,
                                            ALU.add).then_inc(var_ready, 1)
                    pool.wait_ge(var_ready, n + 1)
                    nc.gpsimd.tensor_tensor(rstd[:, :], var_eps[:, :], minus_half.to_broadcast([P, NT]),
                                            ALU.pow).then_inc(rstd_ready, 1)

                def iteration(i, project, attend, finish, even=False):
                    if project:
                        masked_queries(i + 1, 1 - parity(i, even), 0)
                        if not isinstance(i, int) or i + 2 < NB:
                            inverse_deviation(i + 2)
                pool.wait_ge(w_loaded, 96)
                inverse_deviation(0)
                schedule(pool, iteration)

            @block.scalar
            def _(act):
                def iteration(i, project, attend, finish, even=False):
                    n = i + 1
                    if project:
                        act.wait_ge(xnT_ps, n + 1)
                        nc.scalar.copy(xnT[:, :], X[0][:, 0:S]).then_inc(xnT_ready, 1)
                        act.wait_ge(proj_ps, 4 * n + 1)
                        wait(act, stack_ready, 4 * n - 1)
                        nc.scalar.copy(hi[:, 0, :, :].rearrange("p c s -> p (c s)"), X[1][:, :]).then_inc(hi_ready, 1)
                    if attend:
                        act.wait_ge(maxT_ps, i + 1)
                        nc.scalar.copy(maxT[:, 0, :], X[2][0:H, 0:S]).then_inc(max_hi, 1)
                    if project:
                        for j, bank in ((1, 3), (2, 2), (3, 0)):
                            act.wait_ge(proj_ps, 4 * n + j + 1)
                            wait(act, stack_ready, 4 * n + j - 1)
                            nc.scalar.copy(hi[:, j % 2, :, :].rearrange("p c s -> p (c s)"), X[bank][:, :]).then_inc(hi_ready, 1)
                            if finish and j == 2:
                                act.wait_ge(onT_ps, i)
                                nc.scalar.copy(onT[:, :], X[3][:, 0:S]).then_inc(onT_ready, 1)
                        act.wait_ge(v_ps, n + 1)
                        nc.scalar.copy(va[:, 1 - parity(i, even), :, :, 0:HD],
                                       X[2][:, 0:S].rearrange("p (t h d) -> p t h d", t=NT, h=H)).then_inc(v_ready, 1)
                    elif finish:
                        act.wait_ge(onT_ps, i)
                        nc.scalar.copy(onT[:, :], X[3][:, 0:S]).then_inc(onT_ready, 1)
                    if attend:
                        for u in range(6):
                            act.wait_ge(s2_ps, 6 * i + u + 1)
                            if u < 2:
                                wait(act, pv_ps, 4 * i)
                                dst = pk1[:, 8 * u:8 * u + 8, :].rearrange("p (b h) q -> p b (h q)", b=2)
                            else:
                                wait(act, pv_ps, 4 * i + u - 3)
                                dst = pk0[:, u % 2, :, :].rearrange("p (b h) q -> p b (h q)", b=2)
                            nc.scalar.activation(dst, s2[:, :, :], ACT.Exp).then_inc(exp_ready, 1)
                            if u >= 4:
                                evacuate(i, u - 4)
                        evacuate(i, 2)
                        evacuate(i, 3)

                def evacuate(i, c):
                    act.wait_ge(pv_ps, 4 * i + c + 1)
                    wait(act, oq_ps, 2 * i)
                    nc.scalar.copy(oT[:, c, :], X[(3, 0, 1, 2)[c]][:, 0:S]).then_inc(oT_ready, 1)
                schedule(act, iteration)

            @block.vector
            def _(dve):
                def layer_stats(n):
                    for t in range(NT):
                        nc.vector.bn_stats(stats[:, t, :], xs[:, NT * n + t, :]).then_inc(bn, 1)
                    dve.wait_ge(bn, 2 * n + 2)
                    dve.sem_inc(turn_a, 1)
                    for t in range(NT):
                        last = nc.vector.bn_aggr(mean_var[:, t, :], stats[:, t, :])
                    last.then_inc(stats_ready, 1)

                def normalise(n):
                    dve.wait_ge(rstd_ready, n + 1)
                    wait(dve, xnT_ps, n)
                    for t in range(NT):
                        last = nc.vector.tensor_scalar(xn[:, t, :], xs[:, NT * n + t, :], mean_var[:, t, 0:1],
                                                       rstd[:, t:t + 1], ALU.subtract, ALU.mult)
                    last.then_inc(xn_ready, 1)

                def stack(n, j, bank, par):
                    dve.wait_ge(hi_ready, 4 * n + j + 1)
                    if j == 0:
                        wait(dve, s2_ps, 6 * (n - 1))
                    if j == 2:
                        wait(dve, qm_ready, n)
                        wait(dve, s1_ps, 6 * n)
                    dst = ks[:, par, 2 * j:2 * j + 2, :] if j < 2 else qs[:, 2 * j - 4:2 * j - 2, :]
                    nc.vector.scalar_tensor_tensor(dst, hi[:, j % 2, :, :].bitcast(fp32), lo_rows_k if j < 2 else lo_rows_q,
                                                   X[bank][:, :].rearrange("p (c s) -> p c s", c=2), ALU.mult,
                                                   ALU.add).then_inc(stack_ready, 1)

                nc.vector.memset(km[:, :, :, :].bitcast(fp32), 0.0)
                dve.wait_ge(w_loaded, 96)
                nc.vector.tensor_scalar(wq[:, :, :], wq[:, :, :], QK_SCALE, None, ALU.mult).then_inc(wq_scaled, 1)
                dve.wait_ge(x_loaded, 16 * NB)
                layer_stats(0)
                normalise(0)

                def iteration(i, project, attend, finish, even=False):
                    n, par = i + 1, 1 - parity(i, even)
                    if project:
                        stack(n, 0, 1, par)
                    if attend:
                        dve.wait_ge(max_hi, i + 1)
                        nc.vector.tensor_tensor(maxT[:, 1, :], X[2][0:H, 0:S], maxT[:, 0, :].bitcast(fp32),
                                                ALU.subtract).then_inc(maxT_ready, 1)
                    if project:
                        stack(n, 1, 3, par)
                    if finish:
                        dve.wait_ge(oq_ps, 2 * i)
                        for t in range(NT):
                            o = X[t][:, :].rearrange("p (h e) -> p h e", h=H)
                            nc.vector.reciprocal(rden[:, t, :], o[:, :, HD]).then_inc(rden_ready, 1)
                        dve.wait_ge(rden_ready, 2 * i)
                        for t in range(NT):
                            o = X[t][:, :].rearrange("p (h e) -> p h e", h=H)
                            last = nc.vector.tensor_tensor(on[:, t, :, :], o[:, :, 0:HD],
                                                           rden[:, t, :].unsqueeze(2).to_broadcast([P, H, HD]), ALU.mult)
                        last.then_inc(on_ready, 1)
                    if project:
                        dve.wait_ge(stack_ready, 4 * n + 2)
                        wait(dve, s1_ps, 6 * n)
                        for g in range(NG):
                            last = nc.vector.tensor_copy(km[32 * g:32 * g + 32, :, g, :], ks[32 * g:32 * g + 32, par, :, :])
                        last.then_inc(km_ready, 1)
                        stack(n, 2, 2, par)
                        stack(n, 3, 0, par)
                    if finish:
                        dve.wait_ge(y_ps, i)
                        xt = xs[:, bass.ds(NT * (i - 1), NT), :]
                        nc.vector.tensor_tensor(xt, X[1][:, 0:S].rearrange("p (t d) -> p t d", t=NT), xt,
                                                ALU.add).then_inc(x1_ready, 1)
                        dve.wait_ge(x1_ready, i)
                        dve.sem_inc(turn_a, 1)
                        for t in range(NT):
                            nc.vector.bn_stats(stats1[:, t, :], xs[:, bass.ds(NT * (i - 1) + t, 1), :]
                                               .rearrange("p a d -> p (a d)")).then_inc(bn1, 1)
                        dve.wait_ge(bn1, 2 * i)
                        dve.sem_inc(turn_a, 1)
                        for t in range(NT):
                            last = nc.vector.bn_aggr(mv1[:, t, :], stats1[:, t, :])
                        last.then_inc(mv1_ready, 1)
                        dve.wait_ge(mv1_ready, i)
                        nc.vector.tensor_copy(mv_all[:, bass.ds(NT * (i - 1), NT), :], mv1[:, :, :])
                    if project:
                        for u in range(6):
                            dve.wait_ge(s1_ps, 6 * n + u + 1)
                            if u < 2:
                                src = s1[:, :, :].rearrange("p b (g k) -> p (b g) k", k=P)
                                dst = negmax[:, 0, :, 2 * u:2 * u + 2].rearrange("p g c -> p c g")
                            else:
                                src = s1[:, :, :].rearrange("p b (g k) -> p (b g) k", k=S)
                                dst = negmax[:, 1, :, u - 2]
                            wait(dve, maxT_ps, n)
                            nc.vector.tensor_reduce(dst, src, AX.X, ALU.max, negate=True).then_inc(max_ready, 1)
                            if u == 1 and (not isinstance(i, int) or i + 2 < NB):
                                layer_stats(i + 2)
                        if not isinstance(i, int) or i + 2 < NB:
                            normalise(i + 2)
                schedule(dve, iteration)

            @block.tensor
            def _(pe):
                pe.wait_ge(w_loaded, 96)
                pe.wait_ge(wq_scaled, 1)

                def project_pair(n, j, bank):
                    w, const = (wk, const_k) if j < 2 else (wq, const_q)
                    for c in range(2):
                        ch = 2 * (j % 2) + c
                        dst = X[bank][:, c * S:(c + 1) * S]
                        nc.tensor.matmul(dst, const[:, ch, :], pos_rows, start=True, stop=False)
                        last = nc.tensor.matmul(dst, w[:, ch, :], xnT[:, :], start=False, stop=True)
                    last.then_inc(proj_ps, 1)

                def scores_for_max(n, u):
                    pe.wait_ge(max_ready, 6 * n + u) if not isinstance(n, int) or 6 * n + u > 0 else None
                    for b in range(2):
                        if u < 2:
                            c = 2 * u + b
                            nc.tensor.matmul(s1[:, b, :], qs[:, c, 0:P], km[:, c, :, 0:P], start=True, stop=False)
                            last = nc.tensor.matmul(s1[:, b, :], ident_bf, causal, start=False, stop=True)
                        else:
                            c = u - 2
                            nc.tensor.matmul(s1[:, b, :], qs[:, c, P:S], km[:, c, 2 * b:2 * b + 2, :], start=True, stop=False)
                            diag = s1[:, b, :].rearrange("p (g k) -> p g k", g=2)[:, :, P:S]
                            last = nc.tensor.matmul(diag, ident_bf, causal[:, 0:2 * P], start=False, stop=True)
                    last.then_inc(s1_ps, 1)

                def scores_for_exp(i, u, par):
                    if u == 0:
                        pe.wait_ge(max_placed, 128 * (i + 1))
                    wait(pe, exp_ready, 6 * i + u)
                    for b in range(2):
                        if u < 2:
                            c = 2 * u + b
                            nc.tensor.matmul(s2[:, b, :], ks[:, par, c, P:S], qm[par][:, c, :, P:S], start=True, stop=False)
                            last = nc.tensor.matmul(s2[:, b, :], ident_bf, causalT, start=False, stop=True)
                        else:
                            c = u - 2
                            nc.tensor.matmul(s2[:, b, :], ks[:, par, c, 0:P], qm[par][:, c, 2 * b:2 * b + 2, :],
                                             start=True, stop=False)
                            diag = s2[:, b, :].rearrange("p (g q) -> p g q", g=2)[:, :, 0:P]
                            last = nc.tensor.matmul(diag, ident_bf, causalT[:, 0:2 * P], start=False, stop=True)
                    last.then_inc(s2_ps, 1)

                def weigh_values(i, c, par, bank):
                    pe.wait_ge(exp_ready, 6 * i + 3 + c)
                    for g in range(NG):
                        nc.tensor.matmul(X[bank][32 * g:32 * g + 32, 0:S], va[:, par, 0, NG * c + g, :], pk0[:, c % 2, g, :],
                                         start=True, stop=False)
                    for g in range(NG):
                        last = nc.tensor.matmul(X[bank][32 * g:32 * g + 32, P:S], va[:, par, 1, NG * c + g, :],
                                                pk1[:, NG * c + g, :], start=False, stop=True)
                    last.then_inc(pv_ps, 1)

                def iteration(i, project, attend, finish, even=False):
                    n, par = i + 1, parity(i, even)
                    if project:
                        wait(pe, oT_ready, 4 * i)
                        pe.wait_ge(xn_ready, n + 1)
                        for t in range(NT):
                            last = nc.tensor.transpose(X[0][:, t * P:(t + 1) * P], xn[:, t, :], ident)
                        last.then_inc(xnT_ps, 1)
                        pe.wait_ge(xnT_ready, n + 1)
                        project_pair(n, 0, 1)
                    if attend:
                        pe.wait_ge(max_ready, 6 * i + 6)
                        wait(pe, oT_ready, 4 * i)
                        for t in range(NT):
                            last = nc.tensor.transpose(X[2][0:H, t * P:(t + 1) * P], negmax[:, t, :, :].rearrange("p g c -> p (g c)"), ident)
                        last.then_inc(maxT_ps, 1)
                    if project:
                        project_pair(n, 1, 3)
                    if finish:
                        pe.wait_ge(oT_ready, 4 * i)
                        if project:
                            pe.wait_ge(stack_ready, 4 * n + 1)
                        for t in range(NT):
                            for c in range(NC):
                                last = nc.tensor.transpose(X[t][:, c * P:(c + 1) * P], oT[:, c, t * P:(t + 1) * P], ident)
                            last.then_inc(oq_ps, 1)
                    if project:
                        if attend:
                            pe.wait_ge(maxT_ready, i + 1)
                        project_pair(n, 2, 2)
                    if finish:
                        pe.wait_ge(on_ready, i)
                        if project:
                            pe.wait_ge(stack_ready, 4 * n + 2)
                        for t in range(NT):
                            last = nc.tensor.transpose(X[3][:, t * P:(t + 1) * P], on[:, t, :, :].rearrange("p h d -> p (h d)"), ident)
                        last.then_inc(onT_ps, 1)
                    if project:
                        project_pair(n, 3, 0)
                    if finish:
                        pe.wait_ge(onT_ready, i)
                        for t in range(NT):
                            last = nc.tensor.matmul(X[1][:, t * D:(t + 1) * D], onT[:, t * P:(t + 1) * P], wo[:, :], start=True, stop=True)
                        last.then_inc(y_ps, 1)
                    if project:
                        pe.wait_ge(stack_ready, 4 * n + 3)
                        for t in range(NT):
                            last = nc.tensor.matmul(X[2][:, t * D:(t + 1) * D], xnT[:, t * P:(t + 1) * P], wv[:, :], start=True, stop=True)
                        last.then_inc(v_ps, 1)
                    if project:
                        pe.wait_ge(km_ready, n + 1)
                        pe.wait_ge(stack_ready, 4 * n + 4)
                    for u in range(6):
                        if attend:
                            scores_for_exp(i, u, par)
                            if u >= 3:
                                if u == 3:
                                    pe.wait_ge(v_ready, n + 1 if project else i + 1)
                                if u == 5 and finish:
                                    pe.wait_ge(x1_ready, i)
                                weigh_values(i, u - 3, par, (3, 0, 1, 2)[u - 3])
                        if project:
                            scores_for_max(n, u)
                    if attend:
                        weigh_values(i, 3, par, 2)
                schedule(pe, iteration)

        with ExitStack() as part_b:
            def sbb(name, shape, dt):
                return part_b.enter_context(nc.sbuf_tensor(name, shape, dt))

            def psb(name, shape, dt=fp32):
                return part_b.enter_context(nc.psum_tensor(name, shape, dt))

            w1 = [[sbb(f"w1{ab}_{part}", [P, E * F], fp32r) for part in ("hi", "lo")] for ab in "ab"]
            w2 = sbb("w2", [P, E, FC * D], fp32)
            b1 = [sbb(f"b1{ab}", [P, E * F], fp32) for ab in "ab"]
            b2 = sbb("b2", [P, E * D], fp32)
            w_stage = sbb("w_stage", [P, 2, F], fp32)
            wg = sbb("wg", [P, E], fp32)
            bg = sbb("bg", [P, E], fp32)
            ln_w = sbb("ln_w", [P, 1], fp32)
            rc = sbb("rc", [P, E + SLOT_TILES], fp32)
            preference, slot_starts = rc[:, 0:E], rc[0:1, E:]
            rb = sbb("rb", [P, 2 * P], bf16)
            before, ones = rb[:, 0:P], rb[:, P:2 * P]

            xf = sbb("xf", [P, 2, NT, D], fp32)
            xfT = sbb("xfT", [P, 2, S], fp32)
            logits = sbb("logits", [P, TILES, E], fp32)
            r = [sbb(f"r{i}", [P, TILES, E], fp32) for i in range(5)]
            top = [sbb(f"top{i}", [P, TILES, E], fp32) for i in range(2)]
            chosen = sbb("chosen", [P, TILES, E], bf16)
            t64 = [sbb(f"t64_{i}", [P, TILES], fp32) for i in range(6)]
            scale = sbb("scale", [P, TILES], fp32)
            weight = sbb("weight", [P, 2, TILES], fp32)
            slot = sbb("slot", [P, 2, TILES], u32)
            count = sbb("count", [P, E], fp32)
            icount = sbb("icount", [P, E], i32)
            padded = sbb("padded", [P, E], fp32)
            base = sbb("base", [P, 2, E], fp32)
            erow = sbb("erow", [1, 2, SLOT_TILES], fp32)
            expert = sbb("expert", [1, SLOT_TILES], i32)
            xrows = sbb("xrows", [P, 2, D], fp32)
            slot_now = sbb("slot_now", [P, 2, 2], u32)

            xg = sbb("xg", [P, 2, D], fp32)
            xhl = sbb("xhl", [P, 2, 2, P], fp32r)
            sa = sbb("sa", [P, 2, F], fp32)
            sbuf_b = sbb("sbb", [P, 2, F], fp32)
            hT = sbb("hT", [P, FC, P], fp32)
            ys = sbb("ys", [P, 2, D], fp32)
            yg = sbb("yg", [P, 2, 2, D], fp32)

            lg_ps = psb("lg_ps", [P, 512])
            cum_ps = psb("cum_ps", [P, 512])
            tot_ps = psb("tot_ps", [P, 512])
            ab_ps = [[psb(f"ab_ps{i}{j}", [P, 512]) for j in range(2)] for i in range(2)]
            xt_ps = psb("xt_ps", [P, 512])
            ht_ps, y_psb = cum_ps, tot_ps

            wb_loaded = sem("wb_loaded")
            stage_loaded = [sem(f"stage_loaded{i}") for i in range(2)]
            w_split = sem("w_split")
            w_hi = sem("w_hi")
            wb_scaled = sem("wb_scaled")
            chain = sem("chain")
            pow_wanted = sem("pow_wanted")
            pow_done = sem("pow_done")
            xf_ready = sem("xf_ready")
            xfT_ps = sem("xfT_ps")
            xfT_ready = sem("xfT_ready")
            lg_done = sem("lg_done")
            lg_taken = sem("lg_taken")
            exp_wanted = sem("exp_wanted")
            exp_done = sem("exp_done")
            chosen_ready = sem("chosen_ready")
            cum_ready = sem("cum_ready")
            routed = sem("routed")
            rows_ready = sem("rows_ready")
            scattered = [sem(f"scattered{i}") for i in range(2)]
            xg_loaded = [sem(f"xg_loaded{i}") for i in range(2)]
            xgT_ps = sem("xgT_ps")
            xhi_ready = sem("xhi_ready")
            xhl_ready = sem("xhl_ready")
            ab_done = sem("ab_done")
            biased = sem("biased")
            silu_ready = sem("silu_ready")
            h_ready = sem("h_ready")
            hT_done = sem("hT_done")
            hT_ready = sem("hT_ready")
            y_done = sem("y_done")
            y_ready = sem("y_ready")
            y_stored = [sem(f"y_stored{i}") for i in range(2)]
            slot_staged = sem("slot_staged")
            gathered = [sem(f"gathered{i}") for i in range(2)]
            mixed = sem("mixed")
            out_stored = sem("out_stored")
            turn = sem("turn")
            half_mixed = sem("half_mixed")

            NW = 2 * E

            def slot_schedule(eng, iteration):
                for j in range(-1, 4):
                    iteration(j // 2, j % 2, nxt=True, mid=j >= 0, last=j >= 2)
                with eng.Fori(2, SLOT_TILES // 2 - 1, 1) as k:
                    iteration(k, 0, nxt=True, mid=True, last=True)
                    iteration(k, 1, nxt=True, mid=True, last=True)
                for j in range(SLOT_TILES - 2, SLOT_TILES + 2):
                    iteration(j // 2, j % 2, nxt=j + 1 < SLOT_TILES, mid=j < SLOT_TILES, last=True)

            block_b = part_b.enter_context(nc.Block())

            @block_b.sync
            def _(sp):
                sp.dma_start(rc[:, :], route_f32).then_inc(wb_loaded, 16)
                sp.dma_start(rb[:, :], route_bf16).then_inc(wb_loaded, 16)
                sp.dma_start(wg[:, :], wg_in).then_inc(wb_loaded, 16)
                sp.dma_start(ln_w[:, :], ln_w_in.rearrange("(p a) -> p a", a=1)).then_inc(wb_loaded, 16)
                sp.dma_start(bg[:, :], bg_in.rearrange("(a e) -> a e", a=1).to_broadcast([P, E])).then_inc(wb_loaded, 16)
                for ab, src in enumerate((b1a_in, b1b_in)):
                    sp.dma_start(b1[ab][:, :], src.rearrange("(a e) f -> a (e f)", a=1).to_broadcast([P, E * F])).then_inc(wb_loaded, 16)
                sp.dma_start(b2[:, :], b2_in.rearrange("(a e) d -> a (e d)", a=1).to_broadcast([P, E * D])).then_inc(wb_loaded, 16)
                sp.dma_start(w2[:, :, :], w2_in).then_inc(wb_loaded, 16)
                for n in range(NW):
                    ab, e = n // E, n % E
                    wait(sp, w_split, n - 1)
                    sp.dma_start(w_stage[:, n % 2, :], (w1a_in, w1b_in)[ab][e]).then_inc(stage_loaded[n % 2], 16)

                def iteration(k, s, nxt, mid, last):
                    j = 2 * k + s
                    if nxt:
                        sn = 1 - s
                        wait(sp, xgT_ps, j)
                        sp.dma_start(xg[:, sn, :], xs_dram[bass.ds((j + 1) * P, P), :]).then_inc(xg_loaded[sn], 16)
                    if last:
                        sp.wait_ge(y_ready, j - 1)
                        sp.dma_start(ys_dram[bass.ds((j - 2) * P, P), :], ys[:, s, :]).then_inc(y_stored[s], 16)
                sp.wait_ge(scattered[0], 32 * TILES // 2)
                sp.wait_ge(scattered[1], 32 * TILES // 2)
                slot_schedule(sp, iteration)
                with sp.Fori(0, NB, 1) as b:
                    sp.wait_ge(mixed, 2 * b + 2)
                    sp.dma_start(out[bass.ds(b, 1)].rearrange("b (t p) d -> p (b t) d", p=P),
                                 xs[:, bass.ds(NT * b, NT), :]).then_inc(out_stored, 16)
                sp.wait_ge(out_stored, 16 * NB)

            @block_b.gpsimd
            def _(pool):
                for n in range(2):
                    pool.wait_ge(pow_wanted, n + 1)
                    nc.gpsimd.tensor_tensor(t64[1 + 2 * n][:, :], t64[2 * n][:, :], minus_half.to_broadcast([P, TILES]),
                                            ALU.pow).then_inc(pow_done, 1)
                pool.wait_ge(zero_filled, 256)
                with pool.Fori(0, TILES // 2, 1) as k:
                    for s in range(2):
                        pool.wait_ge(rows_ready, 2 * k + s + 1)
                        pool.sem_inc(turn, 1)
                        for choice in range(2):
                            nc.gpsimd.indirect_dma_start(
                                xs_dram, bass.IndirectOffsetOnAxis(slot_now[:, s, choice:choice + 1], 0),
                                xrows[:, s, :], None).then_inc(scattered[s], 16)

                def iteration(k, s, nxt, mid, last):
                    j = 2 * k + s
                    if mid:
                        pool.wait_ge(silu_ready, j + 1)
                        pool.wait_ge(biased, 2 * j + 2)
                        nc.gpsimd.tensor_tensor(sbuf_b[:, s, :], sa[:, s, :], sbuf_b[:, s, :], ALU.mult).then_inc(h_ready, 1)
                slot_schedule(pool, iteration)
                pool.wait_ge(y_stored[0], 16 * SLOT_TILES // 2)
                pool.wait_ge(y_stored[1], 16 * SLOT_TILES // 2)
                with pool.Fori(0, TILES // 2, 1) as k:
                    for s in range(2):
                        pool.wait_ge(slot_staged, 2 * k + s + 1)
                        pool.sem_inc(turn, 1)
                        for choice in range(2):
                            nc.gpsimd.indirect_dma_start(
                                yg[:, s, choice, :], None, ys_dram,
                                bass.IndirectOffsetOnAxis(slot_now[:, s, choice:choice + 1], 0)).then_inc(gathered[s], 16)

            @block_b.scalar
            def _(act):
                act.wait_ge(wb_scaled, 1)
                for n in range(NW):
                    ab, e = n // E, n % E
                    act.wait_ge(stage_loaded[n % 2], 16 * (n // 2 + 1))
                    nc.scalar.activation(w1[ab][0][:, e * F:(e + 1) * F], w_stage[:, n % 2, :], ACT.Identity, bias=0.0,
                                         scale=ln_w[:, 0:1]).then_inc(w_hi, 1)
                with act.Fori(0, NB // 2, 1) as k:
                    for s in range(2):
                        act.wait_ge(xfT_ps, 2 * k + s + 1)
                        nc.scalar.copy(xfT[:, s, :], ab_ps[s][0][:, 0:S]).then_inc(xfT_ready, 1)
                act.wait_ge(exp_wanted, 1)
                nc.scalar.activation(t64[5][:, :], t64[4][:, :], ACT.Exp).then_inc(exp_done, 1)

                def iteration(k, s, nxt, mid, last):
                    j = 2 * k + s
                    if last:
                        act.wait_ge(hT_done, j - 1)
                        wait(act, y_done, j - 2)
                        nc.scalar.copy(hT[:, :, :].rearrange("p c t -> p (c t)"), ht_ps[:, :]).then_inc(hT_ready, 1)
                    if nxt:
                        act.wait_ge(xgT_ps, j + 2)
                        wait(act, ab_done, 2 * j)
                        nc.scalar.copy(xhl[:, 1 - s, 0, :], xt_ps[:, 0:P]).then_inc(xhi_ready, 1)
                    if mid:
                        act.wait_ge(biased, 2 * j + 1)
                        nc.scalar.activation(sa[:, s, :], sa[:, s, :], ACT.Silu).then_inc(silu_ready, 1)
                slot_schedule(act, iteration)

            @block_b.vector
            def _(dve):
                links = [0]

                def link(instruction):
                    links[0] += 1
                    instruction.then_inc(chain, 1)
                    dve.wait_ge(chain, links[0])

                tt, ts_, stt = nc.vector.tensor_tensor, nc.vector.tensor_scalar, nc.vector.scalar_tensor_tensor
                dve.wait_ge(wb_loaded, 16 * 9)
                ts_(wg[:, :], wg[:, :], ln_w[:, 0:1], None, ALU.mult).then_inc(wb_scaled, 1)
                for n in range(NW):
                    ab, e = n // E, n % E
                    dve.wait_ge(w_hi, n + 1)
                    stt(w1[ab][1][:, e * F:(e + 1) * F], w_stage[:, n % 2, :], ln_w[:, 0:1],
                        w1[ab][0][:, e * F:(e + 1) * F].bitcast(fp32), ALU.mult, ALU.subtract).then_inc(w_split, 1)
                var = mv_all[:, :, 1]
                ts_(t64[0][:, :], var, EPS, None, ALU.add).then_inc(pow_wanted, 1)
                dve.wait_ge(pow_done, 1)
                link(tt(t64[4][:, :], t64[1][:, :], t64[1][:, :], ALU.mult))
                link(tt(t64[4][:, :], t64[4][:, :], var, ALU.mult))
                ts_(t64[2][:, :], t64[4][:, :], RMS_EPS, None, ALU.add).then_inc(pow_wanted, 1)
                dve.wait_ge(pow_done, 2)
                link(tt(scale[:, :], t64[1][:, :], t64[3][:, :], ALU.mult))

                with dve.Fori(0, NB // 2, 1) as k:
                    for s in range(2):
                        b = 2 * k + s
                        for t in range(NT):
                            last_i = ts_(xf[:, s, t, :], xs[:, bass.ds(NT * b + t, 1), :].rearrange("p a d -> p (a d)"),
                                         mv_all[:, bass.ds(NT * b + t, 1), 0],
                                         scale[:, bass.ds(NT * b + t, 1)], ALU.subtract, ALU.mult)
                        last_i.then_inc(xf_ready, 1)
                    for s in range(2):
                        b = 2 * k + s
                        dve.wait_ge(lg_done, b + 1)
                        tt(logits[:, bass.ds(NT * b, NT), :], (lg_ps, xt_ps)[s][:, 0:NT * E].rearrange("p (t e) -> p t e", t=NT),
                           bg[:, :].unsqueeze(1).to_broadcast([P, NT, E]), ALU.add).then_inc(lg_taken, 1)
                dve.wait_ge(lg_taken, NB)

                def over_e(v):
                    return v.unsqueeze(2).to_broadcast([P, TILES, E])

                pref = preference.unsqueeze(1).to_broadcast([P, TILES, E])
                reduce = nc.vector.tensor_reduce
                lg = logits[:, :, :]
                best = (t64[0], t64[1])
                for choice in range(2):
                    link(reduce(best[choice][:, :], lg, AX.X, ALU.max))
                    link(tt(r[0][:, :, :], lg, over_e(best[choice][:, :]), ALU.is_equal))
                    link(tt(r[0][:, :, :], r[0][:, :, :], pref, ALU.mult))
                    link(reduce(t64[2][:, :], r[0][:, :, :], AX.X, ALU.max))
                    link(tt(top[choice][:, :, :], pref, over_e(t64[2][:, :]), ALU.is_equal))
                    if choice == 0:
                        link(stt(r[1][:, :, :].rearrange("p t e -> p (t e)"), top[0][:, :, :].rearrange("p t e -> p (t e)"), -3e38,
                                 lg.rearrange("p t e -> p (t e)"), ALU.mult, ALU.add))
                        lg = r[1][:, :, :]
                tt(chosen[:, :, :], top[0][:, :, :], top[1][:, :, :], ALU.add).then_inc(chosen_ready, 1)
                tt(t64[4][:, :], best[1][:, :], best[0][:, :], ALU.subtract).then_inc(exp_wanted, 1)
                dve.wait_ge(exp_done, 1)
                link(ts_(t64[3][:, :], t64[5][:, :], 1.0, None, ALU.add))
                link(nc.vector.reciprocal(weight[:, 0, :], t64[3][:, :]))
                link(tt(weight[:, 1, :], weight[:, 0, :], t64[5][:, :], ALU.mult))
                dve.wait_ge(cum_ready, 1)
                flat = lambda a: a[:, :, :].rearrange("p t e -> p (t e)")
                link(nc.vector.tensor_copy(flat(r[2]), tot_ps[:, :]))
                src, dst = r[2], r[3]
                step = 1
                while step < TILES:
                    nc.vector.tensor_copy(dst[:, 0:step, :], src[:, 0:step, :])
                    link(tt(dst[:, step:TILES, :], src[:, step:TILES, :], src[:, 0:TILES - step, :], ALU.add))
                    src, dst = dst, (r[4] if dst is r[3] else r[3])
                    step *= 2
                link(ts_(count[:, :], src[:, TILES - 1, :], float(P - 1), None, ALU.add))
                link(nc.vector.tensor_copy(icount[:, :], count[:, :]))
                link(ts_(icount[:, :], icount[:, :], P.bit_length() - 1, P.bit_length() - 1, ALU.logical_shift_right, ALU.logical_shift_left))
                link(nc.vector.tensor_copy(padded[:, :], icount[:, :]))
                link(nc.vector.memset(base[:, 0, 0:1], 0.0))
                for e in range(E):
                    link(tt(base[:, 1, e:e + 1], base[:, 0, e:e + 1], padded[:, e:e + 1], ALU.add))
                    if e + 1 < E:
                        link(nc.vector.tensor_copy(base[:, 0, e + 1:e + 2], base[:, 1, e:e + 1]))
                other = r[4] if src is r[3] else r[3]
                link(tt(flat(other), flat(src), flat(r[2]), ALU.subtract))
                link(tt(flat(other), cum_ps[:, :], flat(other), ALU.add))
                link(tt(other[:, :, :], other[:, :, :], base[:, 0, :].unsqueeze(1).to_broadcast([P, TILES, E]), ALU.add))
                for choice in range(2):
                    link(tt(r[0][:, :, :], other[:, :, :], top[choice][:, :, :], ALU.mult))
                    link(reduce(t64[2][:, :], r[0][:, :, :], AX.X, ALU.add))
                    link(nc.vector.tensor_copy(slot[:, choice, :], t64[2][:, :]))
                link(nc.vector.memset(erow[:, 0, :], 0.0))
                for e in range(E - 1):
                    link(stt(erow[:, (e + 1) % 2, :], slot_starts, base[0:1, 1, e:e + 1], erow[:, e % 2, :], ALU.is_ge, ALU.add))
                nc.vector.tensor_copy(expert[:, :], erow[:, (E - 1) % 2, :]).then_inc(routed, 1)
                dve.wait_ge(routed, 1)

                def rows(k, s):
                        t = bass.ds(2 * k + s, 1)
                        wait(dve, scattered[s], 32 * k)
                        ts_(xrows[:, s, :], xs[:, t, :].rearrange("p a d -> p (a d)"), mv_all[:, t, 0], scale[:, t],
                            ALU.subtract, ALU.mult)
                        nc.vector.tensor_copy(slot_now[:, s, :].rearrange("p (c a) -> p c a", a=1), slot[:, :, t]).then_inc(rows_ready, 1)
                rows(0, 0)
                rows(0, 1)
                with dve.Fori(1, TILES // 2, 1) as k:
                    rows(k, 0)
                    rows(k, 1)

                def iteration(k, s, nxt, mid, last):
                    j = 2 * k + s
                    if nxt:
                        dve.wait_ge(xhi_ready, j + 2)
                        tt(xhl[:, 1 - s, 1, :], xt_ps[:, 0:P], xhl[:, 1 - s, 0, :].bitcast(fp32), ALU.subtract).then_inc(xhl_ready, 1)
                    if mid:
                        e = dve.value_load(expert[0:1, bass.ds(j, 1)], min_val=0, max_val=E - 1)
                        dve.wait_ge(ab_done, 2 * j + 1)
                        wait(dve, h_ready, j - 1)
                        tt(sa[:, s, :], ab_ps[s][0][:, :], b1[0][:, bass.ds(e * F, F)], ALU.add).then_inc(biased, 1)
                        dve.wait_ge(ab_done, 2 * j + 2)
                        wait(dve, hT_done, j - 1)
                        tt(sbuf_b[:, s, :], ab_ps[s][1][:, :], b1[1][:, bass.ds(e * F, F)], ALU.add).then_inc(biased, 1)
                    if last:
                        e = dve.value_load(expert[0:1, bass.ds(j - 2, 1)], min_val=0, max_val=E - 1)
                        dve.wait_ge(y_done, j - 1)
                        wait(dve, y_stored[s], 16 * (k - 1))
                        tt(ys[:, s, :], y_psb[:, 0:D], b2[:, bass.ds(e * D, D)], ALU.add).then_inc(y_ready, 1)
                slot_schedule(dve, iteration)

                def mix(k, s):
                    t = bass.ds(2 * k + s, 1)
                    dve.wait_ge(gathered[s], 32 * (k + 1))
                    xt = xs[:, t, :].rearrange("p a d -> p (a d)")
                    stt(yg[:, s, 0, :], yg[:, s, 0, :], weight[:, 0, t], xt, ALU.mult, ALU.add).then_inc(half_mixed, 1)
                    dve.wait_ge(half_mixed, 2 * k + s + 1)
                    stt(xt, yg[:, s, 1, :], weight[:, 1, t], yg[:, s, 0, :], ALU.mult, ALU.add).then_inc(mixed, 1)

                def stage(k, s):
                    t = bass.ds(2 * k + s, 1)
                    nc.vector.tensor_copy(slot_now[:, s, :].rearrange("p (c a) -> p c a", a=1), slot[:, :, t]).then_inc(slot_staged, 1)
                for s in range(2):
                    dve.wait_ge(scattered[s], 32 * TILES // 2)
                stage(0, 0)
                stage(0, 1)
                with dve.Fori(1, TILES // 2, 1) as k:
                    for s in range(2):
                        mix(k - 1, s)
                        stage(k, s)
                for s in range(2):
                    mix(TILES // 2 - 1, s)

            @block_b.tensor
            def _(pe):
                pe.wait_ge(wb_scaled, 1)
                with pe.Fori(0, NB // 2, 1) as k:
                    for s in range(2):
                        b = 2 * k + s
                        pe.wait_ge(xf_ready, b + 1)
                        for t in range(NT):
                            last_i = nc.tensor.transpose(ab_ps[s][0][:, t * P:(t + 1) * P], xf[:, s, t, :], ident)
                        last_i.then_inc(xfT_ps, 1)
                    for s in range(2):
                        b = 2 * k + s
                        pe.wait_ge(xfT_ready, b + 1)
                        for t in range(NT):
                            last_i = nc.tensor.matmul((lg_ps, xt_ps)[s][:, t * E:(t + 1) * E], xfT[:, s, t * P:(t + 1) * P],
                                                      wg[:, :], start=True, stop=True)
                        last_i.then_inc(lg_done, 1)
                pe.wait_ge(chosen_ready, 1)
                rhs = chosen[:, :, :].rearrange("p t e -> p (t e)")
                nc.tensor.matmul(cum_ps[:, :], before, rhs, start=True, stop=True)
                nc.tensor.matmul(tot_ps[:, :], ones, rhs, start=True, stop=True).then_inc(cum_ready, 1)
                pe.wait_ge(routed, 1)
                pe.wait_ge(w_split, NW)

                def iteration(k, s, nxt, mid, last):
                    j = 2 * k + s
                    if last:
                        pe.wait_ge(h_ready, j - 1)
                        wait(pe, hT_ready, j - 2)
                        for c in range(FC):
                            last_i = nc.tensor.transpose(ht_ps[:, c * P:(c + 1) * P], sbuf_b[:, s, c * P:(c + 1) * P], ident)
                        last_i.then_inc(hT_done, 1)
                    if nxt:
                        wait(pe, xhl_ready, j + 1)
                        pe.wait_ge(xg_loaded[1 - s], 16 * (k + s + 1))
                        nc.tensor.transpose(xt_ps[:, 0:P], xg[:, 1 - s, :], ident).then_inc(xgT_ps, 1)
                    if mid:
                        e = pe.value_load(expert[0:1, bass.ds(j, 1)], min_val=0, max_val=E - 1)
                        pe.wait_ge(xhl_ready, j + 1)
                        wait(pe, biased, 2 * j - 2)
                        for ab in range(2):
                            for m, (xpart, wpart) in enumerate(((0, 0), (0, 1), (1, 0))):
                                last_i = nc.tensor.matmul(ab_ps[s][ab][:, :], xhl[:, s, xpart, :],
                                                          w1[ab][wpart][:, bass.ds(e * F, F)], start=m == 0, stop=m == 2)
                            last_i.then_inc(ab_done, 1)
                    if last:
                        e = pe.value_load(expert[0:1, bass.ds(j - 2, 1)], min_val=0, max_val=E - 1)
                        pe.wait_ge(hT_ready, j - 1)
                        wait(pe, y_ready, j - 2)
                        for c in range(FC):
                            last_i = nc.tensor.matmul(y_psb[:, 0:D], hT[:, c, :], w2[:, bass.ds(e, 1), c * D:(c + 1) * D].rearrange("p a d -> p (a d)"),
                                                      start=c == 0, stop=c == FC - 1)
                        last_i.then_inc(y_done, 1)
                slot_schedule(pe, iteration)


def bf16_parts(value, np, bf16):
    high = float(np.float32(value).astype(bf16))
    return high, value - high


def layout_constants():
    import math
    import numpy as np
    bf16 = np.dtype("bfloat16")
    P, S, NC, NG, H, E, TILES = 128, 256, 4, 4, 16, 8, 64
    row = np.arange(P) % 32
    f32 = np.zeros((P, 3 + P), np.float32)
    f32[:, 0] = -0.5
    f32[:, 1] = np.where((row >= 20) & (row < 28), -1, 0)
    f32[:, 2] = np.where((row >= 12) & (row < 20), -1, 0)
    f32[:, 3:] = np.eye(P)
    q = np.arange(P)
    causal = np.where(q[None, :] <= q[:, None], 0, -1e30)
    pos = np.zeros((P, S))
    pos[0] = np.arange(S)
    pos[1:3] = 1
    const_q, const_k = np.zeros((2, P, NC, P))
    h = np.arange(1, H + 1, dtype=np.float32)
    slopes = (np.float32(1) / np.power(np.float32(256), h / np.float32(H))).astype(np.float32)
    for c in range(NC):
        for g in range(NG):
            slope = float(slopes[NG * c + g])
            m, e = math.frexp(slope)
            high = math.ldexp(round(m * 4096), e - 12)
            for base, part in ((0, high), (2, slope - high)):
                p0, p1 = bf16_parts(part, np, bf16)
                const_q[1, c, 32 * g + base], const_q[2, c, 32 * g + base] = p0, p1
                const_q[0, c, 32 * g + base + 1] = -1
                const_k[0, c, 32 * g + base] = 1
                const_k[1, c, 32 * g + base + 1], const_k[2, c, 32 * g + base + 1] = p0, p1
            const_k[1, c, 32 * g + 28] = const_k[1, c, 32 * g + 29] = 1
    b16 = np.concatenate([np.eye(P), np.tile(causal, (1, 4)), np.tile(causal.T, (1, 4)), pos,
                          const_q.reshape(P, -1), const_k.reshape(P, -1)], 1).astype(bf16)
    route = np.concatenate([np.tile(E - np.arange(E), (P, 1)), np.tile(P * np.arange(2 * TILES + E), (P, 1))],
                           1).astype(np.float32)
    route16 = np.concatenate([q[:, None] < q[None, :], np.ones((P, P))], 1).astype(bf16)
    return f32, b16, route, route16


def wide(w, np):
    out = np.zeros((128, 4, 4, 32), w.dtype)
    wt = w.T.reshape(128, 4, 4, 8)
    for copy in range(3):
        out[:, :, :, 4 + 8 * copy:12 + 8 * copy] = wt
    return out.reshape(128, 4, 128)


def kernel(L0_attn_x, L0_attn_W_Q, L0_attn_W_K, L0_attn_W_V, L0_attn_W_O, L0_ffn_ln_w, L0_ffn_Wg, L0_ffn_bg, L0_ffn_W1a,
           L0_ffn_b1a, L0_ffn_W1b, L0_ffn_b1b, L0_ffn_W2, L0_ffn_b2):
    import numpy as np
    import concourse.bacc as bacc
    from concourse.bass_utils import run_bass_kernel_spmd

    f32, b16, route, route16 = layout_constants()
    E, F, D = L0_ffn_W2.shape
    w2 = np.asarray(L0_ffn_W2).reshape(E, F // 128, 128, D).transpose(2, 0, 1, 3).reshape(128, E, F // 128 * D)
    ins = [L0_attn_x, wide(np.asarray(L0_attn_W_Q), np), wide(np.asarray(L0_attn_W_K), np), np.asarray(L0_attn_W_V).T,
           np.asarray(L0_attn_W_O).T, f32, b16, L0_ffn_ln_w, L0_ffn_Wg, L0_ffn_bg, L0_ffn_W1a, L0_ffn_b1a, L0_ffn_W1b,
           L0_ffn_b1b, w2, L0_ffn_b2, route, route16]
    nc = bacc.Bacc("TRN2", target_bir_lowering=False, num_devices=1)
    arrays, args = {}, []
    for n, a in enumerate(ins):
        a = np.ascontiguousarray(a)
        arrays[f"in_{n}_dram"] = a
        args.append(nc.dram_tensor(f"in_{n}_dram", a.shape, mybir.dt.from_np(a.dtype), kind="ExternalInput").ap())
    args.append(nc.dram_tensor("out_0_dram", L0_attn_x.shape, mybir.dt.float32, kind="ExternalOutput").ap())
    build_program(nc, *args)
    r = run_bass_kernel_spmd(nc, [arrays], core_ids=[0])
    return r.results[0]["out_0_dram"]
```

```python
import concourse.bass as bass
from concourse import mybir
from contextlib import ExitStack


def build_program(nc, x_in, wq_in, wk_in, wv_in, wo_in, const_f32, const_bf16, ln_w_in, wg_in, bg_in, w1a_in, b1_in,
                  w1b_in, w2_in, b2_in, route_f32, route_bf16, fill_in, result_rows_in, out):
    fp32 = mybir.dt.float32
    fp32r = mybir.dt.float32r
    bf16 = mybir.dt.bfloat16
    i32, u32 = mybir.dt.int32, mybir.dt.uint32
    ALU = mybir.AluOpType
    ACT = mybir.ActivationFunctionType
    AX = mybir.AxisListType

    P = 128
    NB, S, D = x_in.shape
    H, HD = 16, 8
    NT = S // P
    NC, NG = 4, 4
    TILES = NB * NT
    EPS = 1e-5
    RMS_EPS = 2.0 ** -23
    E, _, F = w1a_in.shape
    FC = F // P
    CHUNK = 4 * P
    SLOT_TILES = 2 * TILES * P // CHUNK + E - 1
    FILLS = 8
    ROW = D + 4
    QK_SCALE = float(HD) ** -0.5

    ctx = ExitStack()
    with ctx:
        def sb(name, shape, dt):
            return ctx.enter_context(nc.sbuf_tensor(name, shape, dt))

        def sem(name):
            return ctx.enter_context(nc.semaphore(name))

        xs = sb("xs", [P, TILES, D], fp32)
        cf = sb("cf", [P, 3 + P], fp32)
        minus_half, lo_rows_q, lo_rows_k = cf[:, 0:1], cf[:, 1:2], cf[:, 2:3]
        ident = cf[:, 3:3 + P]
        mv_all = sb("mv_all", [P, TILES, 2], fp32)
        xs_dram = nc.dram_tensor("expert_inputs", [(SLOT_TILES + 1) * CHUNK, ROW], fp32, kind="Internal").ap()
        ys_dram = nc.dram_tensor("expert_outputs", [2 * TILES * P + FILLS * P, D], fp32, kind="Internal").ap()
        zero_filled = sem("zero_filled")

        def wait(eng, semaphore, value):
            if not isinstance(value, int) or value > 0:
                eng.wait_ge(semaphore, value)

        with ExitStack() as part_a:
            def sba(name, shape, dt):
                return part_a.enter_context(nc.sbuf_tensor(name, shape, dt))

            wq = sba("wq", [P, NC, P], fp32)
            wk = sba("wk", [P, NC, P], fp32)
            wv = sba("wv", [P, D], fp32)
            wo = sba("wo", [P, D], fp32)
            cb = sba("cb", [P, P + 8 * P + S + 2 * NC * P], bf16)
            causalT = cb[:, 5 * P:9 * P]
            ident_bf = cb[:, 0:P]
            causal = cb[:, P:5 * P]
            pos_rows = cb[:, 9 * P:9 * P + S]
            const_q = cb[:, 9 * P + S:9 * P + S + NC * P].rearrange("p (c m) -> p c m", c=NC)
            const_k = cb[:, 9 * P + S + NC * P:].rearrange("p (c m) -> p c m", c=NC)

            stats = sba("stats", [P, NT, 6], fp32)
            mean_var = sba("mean_var", [P, NT, 2], fp32)
            var_eps = sba("var_eps", [P, NT], fp32)
            rstd = sba("rstd", [P, NT], fp32)
            xn = sba("xn", [P, NT, D], fp32)
            xnT = sba("xnT", [P, S], fp32)
            hi = sba("hi", [P, 2, 2, S], fp32r)
            qs = sba("qs", [P, NC, S], fp32r)
            ks = sba("ks", [P, 2, NC, S], fp32r)
            qm = [sba(f"qm{i}", [P, NC, NG, S], fp32r) for i in range(2)]
            km = sba("km", [P, NC, NG, S], fp32r)
            va = sba("va", [P, 2, NT, H, 32], fp32)
            negmax = sba("negmax", [P, NT, NG, NC], fp32)
            maxT = sba("maxT", [H, 2, S], fp32r)
            pk0 = sba("pk0", [P, 2, NG, S], fp32)
            pk1 = sba("pk1", [P, H, P], fp32)
            oT = sba("oT", [P, NC, S], fp32)
            rden = sba("rden", [P, NT, H], fp32)
            on = sba("on", [P, NT, H, HD], fp32)
            onT = sba("onT", [P, S], fp32)

            empty_slots = sba("empty_slots", [P, FILLS, ROW], fp32)
            mv1 = sba("mv1", [P, NT, 2], fp32)
            stats1 = sba("stats1", [P, NT, 6], fp32)
            bn1 = sem("bn1")
            mv1_ready = sem("mv1_ready")
            turn_a = sem("turn_a")
            turn_p = sem("turn_p")
            s1 = part_a.enter_context(nc.psum_tensor("s1", [P, 2, 512], fp32))
            s2 = part_a.enter_context(nc.psum_tensor("s2", [P, 2, 512], fp32))
            X = [part_a.enter_context(nc.psum_tensor(f"x{i}", [P, 512], fp32)) for i in range(4)]

            x_loaded = sem("x_loaded")
            w_loaded = sem("w_loaded")
            wq_scaled = sem("wq_scaled")
            zeroed = sem("zeroed")
            bn = sem("bn")
            stats_ready = sem("stats_ready")
            var_ready = sem("var_ready")
            rstd_ready = sem("rstd_ready")
            xn_ready = sem("xn_ready")
            xnT_ps = sem("xnT_ps")
            xnT_ready = sem("xnT_ready")
            proj_ps = sem("proj_ps")
            hi_ready = sem("hi_ready")
            stack_ready = sem("stack_ready")
            km_ready = sem("km_ready")
            qm_ready = sem("qm_ready")
            v_ps = sem("v_ps")
            v_ready = sem("v_ready")
            s1_ps = sem("s1_ps")
            max_ready = sem("max_ready")
            maxT_ps = sem("maxT_ps")
            max_hi = sem("max_hi")
            maxT_ready = sem("maxT_ready")
            max_placed = sem("max_placed")
            s2_ps = sem("s2_ps")
            exp_ready = sem("exp_ready")
            pv_ps = sem("pv_ps")
            oT_ready = sem("oT_ready")
            oq_ps = sem("oq_ps")
            rden_ready = sem("rden_ready")
            on_ready = sem("on_ready")
            onT_ps = sem("onT_ps")
            onT_ready = sem("onT_ready")
            y_ps = sem("y_ps")
            x1_ready = sem("x1_ready")
            stored = sem("stored")

            def schedule(eng, iteration):
                iteration(-1, project=True, attend=False, finish=False)
                iteration(0, project=True, attend=True, finish=False)
                with eng.Fori(1, NB - 3, 2) as i:
                    iteration(i, project=True, attend=True, finish=True)
                    iteration(i + 1, project=True, attend=True, finish=True, even=True)
                iteration(NB - 3, project=True, attend=True, finish=True)
                iteration(NB - 2, project=True, attend=True, finish=True)
                iteration(NB - 1, project=False, attend=True, finish=True)
                iteration(NB, project=False, attend=False, finish=True)

            def parity(i, even):
                return i % 2 if isinstance(i, int) else (0 if even else 1)

            block = part_a.enter_context(nc.Block())

            @block.sync
            def _(sp):
                sp.dma_start(cf[:, :], const_f32).then_inc(w_loaded, 16)
                sp.dma_start(cb[:, :], const_bf16).then_inc(w_loaded, 16)
                sp.dma_start(empty_slots[:, :, :], fill_in).then_inc(w_loaded, 16)
                sp.dma_start(wq[:, :, :], wq_in).then_inc(w_loaded, 16)
                sp.dma_start(wk[:, :, :], wk_in).then_inc(w_loaded, 16)
                sp.dma_start(wv[:, :], wv_in).then_inc(w_loaded, 16)
                sp.dma_start(wo[:, :], wo_in).then_inc(w_loaded, 16)
                for b in range(NB):
                    sp.dma_start(xs[:, NT * b:NT * b + NT, :], x_in[b].rearrange("(t p) d -> p t d", p=P)).then_inc(x_loaded, 16)

                sp.wait_ge(w_loaded, 112)
                fill = xs_dram.rearrange("(n s p) r -> n p s r", p=P, s=FILLS)
                for n in range((SLOT_TILES + 1) * CHUNK // (FILLS * P)):
                    sp.dma_start(fill[n], empty_slots[:, :, :]).then_inc(zero_filled, 16)

                def iteration(i, project, attend, finish, even=False):
                    if attend:
                        sp.wait_ge(qm_ready, i + 1)
                        sp.wait_ge(maxT_ready, i + 1)
                        for g in range(NG):
                            for part in range(2):
                                row = 32 * g + 28 + part
                                sp.dma_start(qm[parity(i, even)][row:row + 1, :, g, :].bitcast(fp32),
                                             maxT[NC * g:NC * g + NC, part, :].bitcast(fp32)).then_inc(max_placed, 16)
                schedule(sp, iteration)
                sp.wait_ge(zero_filled, 16 * ((SLOT_TILES + 1) * CHUNK // (FILLS * P)))

            @block.gpsimd
            def _(pool):
                def masked_queries(n, par, done):
                    pool.wait_ge(stack_ready, 4 * n + 4)
                    wait(pool, s2_ps, 6 * (n - 1))
                    pool.wait_ge(rstd_ready, n + 1)
                    pool.sem_inc(turn_p, 1)
                    for g in range(NG):
                        last = nc.gpsimd.tensor_scalar(qm[par][32 * g:32 * g + 32, :, g, :],
                                                       qs[32 * g:32 * g + 32, :, :].bitcast(fp32), 1.0, 0.0,
                                                       ALU.mult, ALU.add)
                    last.then_inc(qm_ready, 1)

                def zero(buf):
                    return nc.gpsimd.memset(buf.bitcast(fp32), 0.0)

                zero(qm[0][:, :, :, :])
                zero(qm[1][:, :, :, :])
                nc.gpsimd.memset(va[:, :, :, :, :].rearrange("p a t h e -> p (a t h e)"), 0.0).then_inc(zeroed, 1)
                pool.wait_ge(zeroed, 1)
                nc.gpsimd.memset(va[:, :, :, :, HD:HD + 1], 1.0).then_inc(zeroed, 1)

                def inverse_deviation(n):
                    pool.wait_ge(stats_ready, n + 1)
                    wait(pool, qm_ready, n)
                    pool.sem_inc(turn_p, 1)
                    nc.gpsimd.tensor_scalar(var_eps[:, :], mean_var[:, :, 1], 1.0, EPS, ALU.mult,
                                            ALU.add).then_inc(var_ready, 1)
                    pool.wait_ge(var_ready, n + 1)
                    nc.gpsimd.tensor_tensor(rstd[:, :], var_eps[:, :], minus_half.to_broadcast([P, NT]),
                                            ALU.pow).then_inc(rstd_ready, 1)

                def iteration(i, project, attend, finish, even=False):
                    if project:
                        masked_queries(i + 1, 1 - parity(i, even), 0)
                        if not isinstance(i, int) or i + 2 < NB:
                            inverse_deviation(i + 2)
                pool.wait_ge(w_loaded, 112)
                inverse_deviation(0)
                schedule(pool, iteration)

            @block.scalar
            def _(act):
                def iteration(i, project, attend, finish, even=False):
                    n = i + 1
                    if project:
                        act.wait_ge(xnT_ps, n + 1)
                        nc.scalar.copy(xnT[:, :], X[0][:, 0:S]).then_inc(xnT_ready, 1)
                        act.wait_ge(proj_ps, 4 * n + 1)
                        wait(act, stack_ready, 4 * n - 1)
                        nc.scalar.copy(hi[:, 0, :, :].rearrange("p c s -> p (c s)"), X[1][:, :]).then_inc(hi_ready, 1)
                    if attend:
                        act.wait_ge(maxT_ps, i + 1)
                        nc.scalar.copy(maxT[:, 0, :], X[2][0:H, 0:S]).then_inc(max_hi, 1)
                    if project:
                        for j, bank in ((1, 3), (2, 2), (3, 0)):
                            act.wait_ge(proj_ps, 4 * n + j + 1)
                            wait(act, stack_ready, 4 * n + j - 1)
                            nc.scalar.copy(hi[:, j % 2, :, :].rearrange("p c s -> p (c s)"), X[bank][:, :]).then_inc(hi_ready, 1)
                            if finish and j == 2:
                                act.wait_ge(onT_ps, i)
                                nc.scalar.copy(onT[:, :], X[3][:, 0:S]).then_inc(onT_ready, 1)
                        act.wait_ge(v_ps, n + 1)
                        nc.scalar.copy(va[:, 1 - parity(i, even), :, :, 0:HD],
                                       X[2][:, 0:S].rearrange("p (t h d) -> p t h d", t=NT, h=H)).then_inc(v_ready, 1)
                    elif finish:
                        act.wait_ge(onT_ps, i)
                        nc.scalar.copy(onT[:, :], X[3][:, 0:S]).then_inc(onT_ready, 1)
                    if attend:
                        for u in range(6):
                            act.wait_ge(s2_ps, 6 * i + u + 1)
                            if u < 2:
                                wait(act, pv_ps, 4 * i)
                                dst = pk1[:, 8 * u:8 * u + 8, :].rearrange("p (b h) q -> p b (h q)", b=2)
                            else:
                                wait(act, pv_ps, 4 * i + u - 3)
                                dst = pk0[:, u % 2, :, :].rearrange("p (b h) q -> p b (h q)", b=2)
                            nc.scalar.activation(dst, s2[:, :, :], ACT.Exp).then_inc(exp_ready, 1)
                            if u >= 4:
                                evacuate(i, u - 4)
                        evacuate(i, 2)
                        evacuate(i, 3)

                def evacuate(i, c):
                    act.wait_ge(pv_ps, 4 * i + c + 1)
                    wait(act, oq_ps, 2 * i)
                    nc.scalar.copy(oT[:, c, :], X[(3, 0, 1, 2)[c]][:, 0:S]).then_inc(oT_ready, 1)
                schedule(act, iteration)

            @block.vector
            def _(dve):
                def layer_stats(n):
                    for t in range(NT):
                        nc.vector.bn_stats(stats[:, t, :], xs[:, NT * n + t, :]).then_inc(bn, 1)
                    dve.wait_ge(bn, 2 * n + 2)
                    dve.sem_inc(turn_a, 1)
                    for t in range(NT):
                        last = nc.vector.bn_aggr(mean_var[:, t, :], stats[:, t, :])
                    last.then_inc(stats_ready, 1)

                def normalise(n):
                    dve.wait_ge(rstd_ready, n + 1)
                    wait(dve, xnT_ps, n)
                    for t in range(NT):
                        last = nc.vector.tensor_scalar(xn[:, t, :], xs[:, NT * n + t, :], mean_var[:, t, 0:1],
                                                       rstd[:, t:t + 1], ALU.subtract, ALU.mult)
                    last.then_inc(xn_ready, 1)

                def stack(n, j, bank, par):
                    dve.wait_ge(hi_ready, 4 * n + j + 1)
                    if j == 0:
                        wait(dve, s2_ps, 6 * (n - 1))
                    if j == 2:
                        wait(dve, qm_ready, n)
                        wait(dve, s1_ps, 6 * n)
                    dst = ks[:, par, 2 * j:2 * j + 2, :] if j < 2 else qs[:, 2 * j - 4:2 * j - 2, :]
                    nc.vector.scalar_tensor_tensor(dst, hi[:, j % 2, :, :].bitcast(fp32), lo_rows_k if j < 2 else lo_rows_q,
                                                   X[bank][:, :].rearrange("p (c s) -> p c s", c=2), ALU.mult,
                                                   ALU.add).then_inc(stack_ready, 1)

                nc.vector.memset(km[:, :, :, :].bitcast(fp32), 0.0)
                dve.wait_ge(w_loaded, 112)
                nc.vector.tensor_scalar(wq[:, :, :], wq[:, :, :], QK_SCALE, None, ALU.mult).then_inc(wq_scaled, 1)
                dve.wait_ge(x_loaded, 16 * NB)
                layer_stats(0)
                normalise(0)

                def iteration(i, project, attend, finish, even=False):
                    n, par = i + 1, 1 - parity(i, even)
                    if project:
                        stack(n, 0, 1, par)
                    if attend:
                        dve.wait_ge(max_hi, i + 1)
                        nc.vector.tensor_tensor(maxT[:, 1, :], X[2][0:H, 0:S], maxT[:, 0, :].bitcast(fp32),
                                                ALU.subtract).then_inc(maxT_ready, 1)
                    if project:
                        stack(n, 1, 3, par)
                    if finish:
                        dve.wait_ge(oq_ps, 2 * i)
                        for t in range(NT):
                            o = X[t][:, :].rearrange("p (h e) -> p h e", h=H)
                            nc.vector.reciprocal(rden[:, t, :], o[:, :, HD]).then_inc(rden_ready, 1)
                        dve.wait_ge(rden_ready, 2 * i)
                        for t in range(NT):
                            o = X[t][:, :].rearrange("p (h e) -> p h e", h=H)
                            last = nc.vector.tensor_tensor(on[:, t, :, :], o[:, :, 0:HD],
                                                           rden[:, t, :].unsqueeze(2).to_broadcast([P, H, HD]), ALU.mult)
                        last.then_inc(on_ready, 1)
                    if project:
                        dve.wait_ge(stack_ready, 4 * n + 2)
                        wait(dve, s1_ps, 6 * n)
                        for g in range(NG):
                            last = nc.vector.tensor_copy(km[32 * g:32 * g + 32, :, g, :], ks[32 * g:32 * g + 32, par, :, :])
                        last.then_inc(km_ready, 1)
                        stack(n, 2, 2, par)
                        stack(n, 3, 0, par)
                    if finish:
                        dve.wait_ge(y_ps, i)
                        xt = xs[:, bass.ds(NT * (i - 1), NT), :]
                        nc.vector.tensor_tensor(xt, X[1][:, 0:S].rearrange("p (t d) -> p t d", t=NT), xt,
                                                ALU.add).then_inc(x1_ready, 1)
                        dve.wait_ge(x1_ready, i)
                        dve.sem_inc(turn_a, 1)
                        for t in range(NT):
                            nc.vector.bn_stats(stats1[:, t, :], xs[:, bass.ds(NT * (i - 1) + t, 1), :]
                                               .rearrange("p a d -> p (a d)")).then_inc(bn1, 1)
                        dve.wait_ge(bn1, 2 * i)
                        dve.sem_inc(turn_a, 1)
                        for t in range(NT):
                            last = nc.vector.bn_aggr(mv1[:, t, :], stats1[:, t, :])
                        last.then_inc(mv1_ready, 1)
                        dve.wait_ge(mv1_ready, i)
                        nc.vector.tensor_copy(mv_all[:, bass.ds(NT * (i - 1), NT), :], mv1[:, :, :])
                    if project:
                        for u in range(6):
                            dve.wait_ge(s1_ps, 6 * n + u + 1)
                            if u < 2:
                                src = s1[:, :, :].rearrange("p b (g k) -> p (b g) k", k=P)
                                dst = negmax[:, 0, :, 2 * u:2 * u + 2].rearrange("p g c -> p c g")
                            else:
                                src = s1[:, :, :].rearrange("p b (g k) -> p (b g) k", k=S)
                                dst = negmax[:, 1, :, u - 2]
                            wait(dve, maxT_ps, n)
                            nc.vector.tensor_reduce(dst, src, AX.X, ALU.max, negate=True).then_inc(max_ready, 1)
                            if u == 1 and (not isinstance(i, int) or i + 2 < NB):
                                layer_stats(i + 2)
                        if not isinstance(i, int) or i + 2 < NB:
                            normalise(i + 2)
                schedule(dve, iteration)

            @block.tensor
            def _(pe):
                pe.wait_ge(w_loaded, 112)
                pe.wait_ge(wq_scaled, 1)

                def project_pair(n, j, bank):
                    w, const = (wk, const_k) if j < 2 else (wq, const_q)
                    for c in range(2):
                        ch = 2 * (j % 2) + c
                        dst = X[bank][:, c * S:(c + 1) * S]
                        nc.tensor.matmul(dst, const[:, ch, :], pos_rows, start=True, stop=False)
                        last = nc.tensor.matmul(dst, w[:, ch, :], xnT[:, :], start=False, stop=True)
                    last.then_inc(proj_ps, 1)

                def scores_for_max(n, u):
                    pe.wait_ge(max_ready, 6 * n + u) if not isinstance(n, int) or 6 * n + u > 0 else None
                    for b in range(2):
                        if u < 2:
                            c = 2 * u + b
                            nc.tensor.matmul(s1[:, b, :], qs[:, c, 0:P], km[:, c, :, 0:P], start=True, stop=False)
                            last = nc.tensor.matmul(s1[:, b, :], ident_bf, causal, start=False, stop=True)
                        else:
                            c = u - 2
                            nc.tensor.matmul(s1[:, b, :], qs[:, c, P:S], km[:, c, 2 * b:2 * b + 2, :], start=True, stop=False)
                            diag = s1[:, b, :].rearrange("p (g k) -> p g k", g=2)[:, :, P:S]
                            last = nc.tensor.matmul(diag, ident_bf, causal[:, 0:2 * P], start=False, stop=True)
                    last.then_inc(s1_ps, 1)

                def scores_for_exp(i, u, par):
                    if u == 0:
                        pe.wait_ge(max_placed, 128 * (i + 1))
                    wait(pe, exp_ready, 6 * i + u)
                    for b in range(2):
                        if u < 2:
                            c = 2 * u + b
                            nc.tensor.matmul(s2[:, b, :], ks[:, par, c, P:S], qm[par][:, c, :, P:S], start=True, stop=False)
                            last = nc.tensor.matmul(s2[:, b, :], ident_bf, causalT, start=False, stop=True)
                        else:
                            c = u - 2
                            nc.tensor.matmul(s2[:, b, :], ks[:, par, c, 0:P], qm[par][:, c, 2 * b:2 * b + 2, :],
                                             start=True, stop=False)
                            diag = s2[:, b, :].rearrange("p (g q) -> p g q", g=2)[:, :, 0:P]
                            last = nc.tensor.matmul(diag, ident_bf, causalT[:, 0:2 * P], start=False, stop=True)
                    last.then_inc(s2_ps, 1)

                def weigh_values(i, c, par, bank):
                    pe.wait_ge(exp_ready, 6 * i + 3 + c)
                    for g in range(NG):
                        nc.tensor.matmul(X[bank][32 * g:32 * g + 32, 0:S], va[:, par, 0, NG * c + g, :], pk0[:, c % 2, g, :],
                                         start=True, stop=False)
                    for g in range(NG):
                        last = nc.tensor.matmul(X[bank][32 * g:32 * g + 32, P:S], va[:, par, 1, NG * c + g, :],
                                                pk1[:, NG * c + g, :], start=False, stop=True)
                    last.then_inc(pv_ps, 1)

                def iteration(i, project, attend, finish, even=False):
                    n, par = i + 1, parity(i, even)
                    if project:
                        wait(pe, oT_ready, 4 * i)
                        pe.wait_ge(xn_ready, n + 1)
                        for t in range(NT):
                            last = nc.tensor.transpose(X[0][:, t * P:(t + 1) * P], xn[:, t, :], ident)
                        last.then_inc(xnT_ps, 1)
                        pe.wait_ge(xnT_ready, n + 1)
                        project_pair(n, 0, 1)
                    if attend:
                        pe.wait_ge(max_ready, 6 * i + 6)
                        wait(pe, oT_ready, 4 * i)
                        for t in range(NT):
                            last = nc.tensor.transpose(X[2][0:H, t * P:(t + 1) * P], negmax[:, t, :, :].rearrange("p g c -> p (g c)"), ident)
                        last.then_inc(maxT_ps, 1)
                    if project:
                        project_pair(n, 1, 3)
                    if finish:
                        pe.wait_ge(oT_ready, 4 * i)
                        if project:
                            pe.wait_ge(stack_ready, 4 * n + 1)
                        for t in range(NT):
                            for c in range(NC):
                                last = nc.tensor.transpose(X[t][:, c * P:(c + 1) * P], oT[:, c, t * P:(t + 1) * P], ident)
                            last.then_inc(oq_ps, 1)
                    if project:
                        if attend:
                            pe.wait_ge(maxT_ready, i + 1)
                        project_pair(n, 2, 2)
                    if finish:
                        pe.wait_ge(on_ready, i)
                        if project:
                            pe.wait_ge(stack_ready, 4 * n + 2)
                        for t in range(NT):
                            last = nc.tensor.transpose(X[3][:, t * P:(t + 1) * P], on[:, t, :, :].rearrange("p h d -> p (h d)"), ident)
                        last.then_inc(onT_ps, 1)
                    if project:
                        project_pair(n, 3, 0)
                    if finish:
                        pe.wait_ge(onT_ready, i)
                        for t in range(NT):
                            last = nc.tensor.matmul(X[1][:, t * D:(t + 1) * D], onT[:, t * P:(t + 1) * P], wo[:, :], start=True, stop=True)
                        last.then_inc(y_ps, 1)
                    if project:
                        pe.wait_ge(stack_ready, 4 * n + 3)
                        for t in range(NT):
                            last = nc.tensor.matmul(X[2][:, t * D:(t + 1) * D], xnT[:, t * P:(t + 1) * P], wv[:, :], start=True, stop=True)
                        last.then_inc(v_ps, 1)
                    if project:
                        pe.wait_ge(km_ready, n + 1)
                        pe.wait_ge(stack_ready, 4 * n + 4)
                    for u in range(6):
                        if attend:
                            scores_for_exp(i, u, par)
                            if u >= 3:
                                if u == 3:
                                    pe.wait_ge(v_ready, n + 1 if project else i + 1)
                                if u == 5 and finish:
                                    pe.wait_ge(x1_ready, i)
                                weigh_values(i, u - 3, par, (3, 0, 1, 2)[u - 3])
                        if project:
                            scores_for_max(n, u)
                    if attend:
                        weigh_values(i, 3, par, 2)
                schedule(pe, iteration)

        with ExitStack() as part_b:
            def sbb(name, shape, dt):
                return part_b.enter_context(nc.sbuf_tensor(name, shape, dt))

            def psb(name, shape, dt=fp32):
                return part_b.enter_context(nc.psum_tensor(name, shape, dt))

            w1 = sbb("w1", [P, E, 2, F], fp32)
            w1_now = sbb("w1_now", [P, 2, 2, 2, F], fp32r)
            w2 = sbb("w2", [P, E * FC * D], fp32)
            b1 = sbb("b1", [P, E, 2 * FC], fp32)
            bias_now = sbb("bias_now", [P, 2, 2 * FC], fp32)
            b2 = sbb("b2", [P, E * D], fp32)
            wg = sbb("wg", [P, E], fp32)
            bg = sbb("bg", [P, E], fp32)
            ln_w = sbb("ln_w", [P, 1], fp32)
            rc = sbb("rc", [P, E + SLOT_TILES + 3], fp32)
            preference, slot_starts = rc[:, 0:E], rc[0:1, E:]
            rb = sbb("rb", [P, 2 * P], bf16)
            before, ones = rb[:, 0:P], rb[:, P:2 * P]

            xf = sbb("xf", [P, 2, NT, D], fp32)
            xfT = sbb("xfT", [P, 2, S], fp32)
            logits = sbb("logits", [P, TILES, E], fp32)
            r = [sbb(f"r{i}", [P, TILES, E], fp32) for i in range(5)]
            top = [sbb(f"top{i}", [P, TILES, E], fp32) for i in range(2)]
            chosen = sbb("chosen", [P, TILES, E], bf16)
            t64 = [sbb(f"t64_{i}", [P, TILES], fp32) for i in range(6)]
            scale = sbb("scale", [P, TILES], fp32)
            weight = sbb("weight", [P, 2, TILES], fp32)
            slot = sbb("slot", [P, 2, TILES], u32)
            count = sbb("count", [P, E], fp32)
            icount = sbb("icount", [P, E], i32)
            padded = sbb("padded", [P, E], fp32)
            base = sbb("base", [P, 2, E], fp32)
            erow = sbb("erow", [1, 2, SLOT_TILES + 3], fp32)
            expert = sbb("expert", [1, SLOT_TILES + 3], i32)
            xrows = sbb("xrows", [P, 2, 2, ROW], fp32)
            slot_now = sbb("slot_now", [P, 2, 2], u32)
            result_row = sbb("result_row", [P, 2, TILES], u32)

            xg = sbb("xg", [P, 2, 4, ROW], fp32)
            result_next = sbb("result_next", [P, 2, 4], u32)
            result_now = sbb("result_now", [P, 2, 4], u32)
            xhl = sbb("xhl", [P, 2, 2, CHUNK], fp32r)
            sa = sbb("sa", [P, 2, CHUNK], fp32)
            hT = sbb("hT", [P, 2, FC, CHUNK], fp32)
            ys = sbb("ys", [P, 2, 4, D], fp32)
            yg = sbb("yg", [P, 4, 2, NT, D], fp32)

            ab_ps = [[psb(f"ab_ps{i}{j}", [P, CHUNK]) for j in range(2)] for i in range(2)]
            y_psb = [psb(f"y_psb{i}", [P, 512]) for i in range(2)]
            xt_ps = psb("xt_ps", [P, CHUNK])
            lg_ps = psb("lg_ps", [P, 512])
            cum_ps, tot_ps = y_psb

            wb_loaded = sem("wb_loaded")
            w_split = sem("w_split")
            w_hi = sem("w_hi")
            wb_scaled = sem("wb_scaled")
            chain = sem("chain")
            pow_wanted = sem("pow_wanted")
            pow_done = sem("pow_done")
            xf_ready = sem("xf_ready")
            xfT_ps = sem("xfT_ps")
            xfT_ready = sem("xfT_ready")
            lg_done = sem("lg_done")
            lg_taken = sem("lg_taken")
            exp_wanted = sem("exp_wanted")
            exp_done = sem("exp_done")
            chosen_ready = sem("chosen_ready")
            cum_ready = sem("cum_ready")
            routed = sem("routed")
            rows_ready = sem("rows_ready")
            scattered = [sem(f"scattered{i}") for i in range(2)]
            xg_loaded = [sem(f"xg_loaded{i}") for i in range(2)]
            xgT_ps = sem("xgT_ps")
            xhi_ready = sem("xhi_ready")
            xhl_ready = sem("xhl_ready")
            ab_done = sem("ab_done")
            bias_ready = sem("bias_ready")
            next_taken = sem("next_taken")
            next_moved = sem("next_moved")
            silu_ready = sem("silu_ready")
            h_ready = sem("h_ready")
            y_done = sem("y_done")
            y_ready = sem("y_ready")
            y_scattered = [sem(f"y_scattered{i}") for i in range(2)]
            y_loaded = [sem(f"y_loaded{i}") for i in range(4)]
            mixed = sem("mixed")
            out_stored = sem("out_stored")
            turn = sem("turn")
            half_mixed = sem("half_mixed")

            def experts(eng, first, n):
                return nc.values_load_multi_w_load_instructions(expert[0:1, bass.ds(first + 1, n)], [eng.engine],
                                                                min_val=0, max_val=E - 1)[1]

            def slot_schedule(eng, iteration, load=True):
                def step(j):
                    e = experts(eng, max(j - 1, -1), 3) if load else None
                    if load and j < 0:
                        e = (None,) + e
                    iteration(j // 2, j % 2, e, nxt=j + 1 < SLOT_TILES, mid=0 <= j < SLOT_TILES, last=j >= 1)
                for j in range(-1, 2):
                    step(j)
                with eng.Fori(1, SLOT_TILES // 2, 1) as k:
                    e = experts(eng, 2 * k - 1, 4) if load else (0,) * 4
                    for s in range(2):
                        iteration(k, s, e[s:s + 3], nxt=True, mid=True, last=True)
                for j in range(SLOT_TILES - 1, SLOT_TILES + 1):
                    step(j)

            block_b = part_b.enter_context(nc.Block())

            @block_b.sync
            def _(sp):
                sp.dma_start(rc[:, :], route_f32).then_inc(wb_loaded, 16)
                sp.dma_start(result_row[:, :, :], result_rows_in).then_inc(wb_loaded, 16)
                sp.dma_start(rb[:, :], route_bf16).then_inc(wb_loaded, 16)
                sp.dma_start(wg[:, :], wg_in).then_inc(wb_loaded, 16)
                sp.dma_start(ln_w[:, :], ln_w_in.rearrange("(p a) -> p a", a=1)).then_inc(wb_loaded, 16)
                sp.dma_start(bg[:, :], bg_in.rearrange("(a e) -> a e", a=1).to_broadcast([P, E])).then_inc(wb_loaded, 16)
                sp.dma_start(b1[:, :, :], b1_in).then_inc(wb_loaded, 16)
                sp.dma_start(b2[:, :], b2_in.rearrange("(a e) d -> a (e d)", a=1).to_broadcast([P, E * D])).then_inc(wb_loaded, 16)
                sp.dma_start(w2[:, :], w2_in).then_inc(wb_loaded, 16)
                for ab, src in enumerate((w1a_in, w1b_in)):
                    sp.dma_start(w1[:, :, ab, :], src.rearrange("e p f -> p e f")).then_inc(wb_loaded, 16)

                for p_ in range(2):
                    sp.wait_ge(scattered[p_], 32 * TILES // 2)

                def load(k, s):
                    j = 2 * k + s
                    wait(sp, xgT_ps, j - 1)
                    wait(sp, next_taken, j - 1)
                    rows = xs_dram[bass.ds(j * CHUNK, CHUNK), :].rearrange("(t p) r -> p t r", p=P)
                    sp.dma_start(xg[:, s, :, :], rows).then_inc(xg_loaded[s], 16)
                load(0, 0)
                load(0, 1)
                with sp.Fori(1, SLOT_TILES // 2, 1) as k:
                    load(k, 0)
                    load(k, 1)
                load(SLOT_TILES // 2, 0)

                sp.wait_ge(y_scattered[0], 64 * ((SLOT_TILES + 1) // 2))
                sp.wait_ge(y_scattered[1], 64 * (SLOT_TILES // 2))

                def load_results(b, m):
                    for choice in range(2):
                        rows = ys_dram[bass.ds(choice * TILES * P + b * S, S), :].rearrange("(t p) d -> p t d", p=P)
                        sp.dma_start(yg[:, m, choice, :, :], rows).then_inc(y_loaded[m], 16)
                for m in range(4):
                    load_results(m, m)
                with sp.Fori(1, NB // 4, 1) as k:
                    for m in range(4):
                        sp.wait_ge(mixed, NT * (4 * k + m - 3))
                        load_results(4 * k + m, m)
                sp.wait_ge(out_stored, 16 * NB)

            @block_b.gpsimd
            def _(pool):
                for n in range(2):
                    pool.wait_ge(pow_wanted, n + 1)
                    nc.gpsimd.tensor_tensor(t64[1 + 2 * n][:, :], t64[2 * n][:, :], minus_half.to_broadcast([P, TILES]),
                                            ALU.pow).then_inc(pow_done, 1)
                pool.wait_ge(zero_filled, 16 * ((SLOT_TILES + 1) * CHUNK // (FILLS * P)))
                with pool.Fori(0, TILES // 2, 1) as k:
                    for s in range(2):
                        pool.wait_ge(rows_ready, 2 * k + s + 1)
                        pool.sem_inc(turn, 1)
                        for choice in range(2):
                            nc.gpsimd.indirect_dma_start(
                                xs_dram, bass.IndirectOffsetOnAxis(slot_now[:, s, choice:choice + 1], 0),
                                xrows[:, s, choice, :], None).then_inc(scattered[s], 16)

                def iteration(k, s, e, nxt, mid, last):
                    if last:
                        pool.wait_ge(y_ready, 2 * k + s)
                        pool.sem_inc(turn, 1)
                        for t in range(4):
                            nc.gpsimd.indirect_dma_start(
                                ys_dram, bass.IndirectOffsetOnAxis(result_now[:, 1 - s, t:t + 1], 0),
                                ys[:, 1 - s, t, :], None).then_inc(y_scattered[1 - s], 16)
                slot_schedule(pool, iteration, load=False)

            @block_b.scalar
            def _(act):
                act.wait_ge(wb_scaled, 1)
                with act.Fori(0, NB // 2, 1) as k:
                    for s in range(2):
                        act.wait_ge(xfT_ps, 2 * k + s + 1)
                        nc.scalar.copy(xfT[:, s, :], ab_ps[s][0][:, 0:S]).then_inc(xfT_ready, 1)
                act.wait_ge(exp_wanted, 1)
                nc.scalar.activation(t64[5][:, :], t64[4][:, :], ACT.Exp).then_inc(exp_done, 1)
                act.wait_ge(routed, 1)

                def iteration(k, s, e, nxt, mid, last):
                    j = 2 * k + s
                    if mid:
                        act.wait_ge(bias_ready, j + 1)
                    for c in range(FC):
                        if mid:
                            act.wait_ge(ab_done, 8 * j + 2 * c + 1)
                            nc.scalar.activation(sa[:, c % 2, :], ab_ps[c % 2][0][:, :], ACT.Silu,
                                                 bias=bias_now[:, s, c:c + 1]).then_inc(silu_ready, 1)
                        if nxt and c == 0:
                            act.wait_ge(xgT_ps, j + 2)
                            wait(act, ab_done, 8 * j)
                            nc.scalar.copy(xhl[:, 1 - s, 0, :], xt_ps[:, :]).then_inc(xhi_ready, 1)
                        if nxt and c == 1:
                            nc.scalar.activation(w1_now[:, 1 - s, 0, :, :].rearrange("p a f -> p (a f)"),
                                                 w1[:, bass.ds(e[2], 1), :, :].rearrange("p e a f -> p (e a f)"),
                                                 ACT.Identity, bias=0.0, scale=ln_w[:, 0:1]).then_inc(w_hi, 1)
                slot_schedule(act, iteration)
                with act.Fori(0, NB, 1) as b:
                    act.wait_ge(mixed, NT * b + NT)
                    act.dma_start(out[bass.ds(b, 1)].rearrange("b (t p) d -> p (b t) d", p=P),
                                  xs[:, bass.ds(NT * b, NT), :]).then_inc(out_stored, 16)

            @block_b.vector
            def _(dve):
                links = [0]

                def link(instruction):
                    links[0] += 1
                    instruction.then_inc(chain, 1)
                    dve.wait_ge(chain, links[0])

                tt, ts_, stt = nc.vector.tensor_tensor, nc.vector.tensor_scalar, nc.vector.scalar_tensor_tensor
                dve.wait_ge(wb_loaded, 16 * 11)
                ts_(wg[:, :], wg[:, :], ln_w[:, 0:1], None, ALU.mult).then_inc(wb_scaled, 1)
                var = mv_all[:, :, 1]
                ts_(t64[0][:, :], var, EPS, None, ALU.add).then_inc(pow_wanted, 1)
                dve.wait_ge(pow_done, 1)
                link(tt(t64[4][:, :], t64[1][:, :], t64[1][:, :], ALU.mult))
                link(tt(t64[4][:, :], t64[4][:, :], var, ALU.mult))
                ts_(t64[2][:, :], t64[4][:, :], RMS_EPS, None, ALU.add).then_inc(pow_wanted, 1)
                dve.wait_ge(pow_done, 2)
                link(tt(scale[:, :], t64[1][:, :], t64[3][:, :], ALU.mult))

                with dve.Fori(0, NB // 2, 1) as k:
                    for s in range(2):
                        b = 2 * k + s
                        for t in range(NT):
                            last_i = ts_(xf[:, s, t, :], xs[:, bass.ds(NT * b + t, 1), :].rearrange("p a d -> p (a d)"),
                                         mv_all[:, bass.ds(NT * b + t, 1), 0],
                                         scale[:, bass.ds(NT * b + t, 1)], ALU.subtract, ALU.mult)
                        last_i.then_inc(xf_ready, 1)
                    for s in range(2):
                        b = 2 * k + s
                        dve.wait_ge(lg_done, b + 1)
                        tt(logits[:, bass.ds(NT * b, NT), :], (lg_ps, xt_ps)[s][:, 0:NT * E].rearrange("p (t e) -> p t e", t=NT),
                           bg[:, :].unsqueeze(1).to_broadcast([P, NT, E]), ALU.add).then_inc(lg_taken, 1)
                dve.wait_ge(lg_taken, NB)

                def over_e(v):
                    return v.unsqueeze(2).to_broadcast([P, TILES, E])

                pref = preference.unsqueeze(1).to_broadcast([P, TILES, E])
                reduce = nc.vector.tensor_reduce
                lg = logits[:, :, :]
                best = (t64[0], t64[1])
                for choice in range(2):
                    link(reduce(best[choice][:, :], lg, AX.X, ALU.max))
                    link(tt(r[0][:, :, :], lg, over_e(best[choice][:, :]), ALU.is_equal))
                    link(tt(r[0][:, :, :], r[0][:, :, :], pref, ALU.mult))
                    link(reduce(t64[2][:, :], r[0][:, :, :], AX.X, ALU.max))
                    link(tt(top[choice][:, :, :], pref, over_e(t64[2][:, :]), ALU.is_equal))
                    if choice == 0:
                        link(stt(r[1][:, :, :].rearrange("p t e -> p (t e)"), top[0][:, :, :].rearrange("p t e -> p (t e)"), -3e38,
                                 lg.rearrange("p t e -> p (t e)"), ALU.mult, ALU.add))
                        lg = r[1][:, :, :]
                tt(chosen[:, :, :], top[0][:, :, :], top[1][:, :, :], ALU.add).then_inc(chosen_ready, 1)
                tt(t64[4][:, :], best[1][:, :], best[0][:, :], ALU.subtract).then_inc(exp_wanted, 1)
                dve.wait_ge(exp_done, 1)
                link(ts_(t64[3][:, :], t64[5][:, :], 1.0, None, ALU.add))
                link(nc.vector.reciprocal(weight[:, 0, :], t64[3][:, :]))
                link(tt(weight[:, 1, :], weight[:, 0, :], t64[5][:, :], ALU.mult))
                dve.wait_ge(cum_ready, 1)
                flat = lambda a: a[:, :, :].rearrange("p t e -> p (t e)")
                link(nc.vector.tensor_copy(flat(r[2]), tot_ps[:, :]))
                src, dst = r[2], r[3]
                step = 1
                while step < TILES:
                    nc.vector.tensor_copy(dst[:, 0:step, :], src[:, 0:step, :])
                    link(tt(dst[:, step:TILES, :], src[:, step:TILES, :], src[:, 0:TILES - step, :], ALU.add))
                    src, dst = dst, (r[4] if dst is r[3] else r[3])
                    step *= 2
                link(ts_(count[:, :], src[:, TILES - 1, :], float(CHUNK - 1), None, ALU.add))
                link(nc.vector.tensor_copy(icount[:, :], count[:, :]))
                link(ts_(icount[:, :], icount[:, :], CHUNK.bit_length() - 1, CHUNK.bit_length() - 1, ALU.logical_shift_right, ALU.logical_shift_left))
                link(nc.vector.tensor_copy(padded[:, :], icount[:, :]))
                link(nc.vector.memset(base[:, 0, 0:1], 0.0))
                for e in range(E):
                    link(tt(base[:, 1, e:e + 1], base[:, 0, e:e + 1], padded[:, e:e + 1], ALU.add))
                    if e + 1 < E:
                        link(nc.vector.tensor_copy(base[:, 0, e + 1:e + 2], base[:, 1, e:e + 1]))
                other = r[4] if src is r[3] else r[3]
                link(tt(flat(other), flat(src), flat(r[2]), ALU.subtract))
                link(tt(flat(other), cum_ps[:, :], flat(other), ALU.add))
                link(tt(other[:, :, :], other[:, :, :], base[:, 0, :].unsqueeze(1).to_broadcast([P, TILES, E]), ALU.add))
                for choice in range(2):
                    link(tt(r[0][:, :, :], other[:, :, :], top[choice][:, :, :], ALU.mult))
                    link(reduce(t64[2][:, :], r[0][:, :, :], AX.X, ALU.add))
                    link(nc.vector.tensor_copy(slot[:, choice, :], t64[2][:, :]))
                link(nc.vector.memset(erow[:, 0, :], 0.0))
                for e in range(E - 1):
                    link(stt(erow[:, (e + 1) % 2, :], slot_starts, base[0:1, 1, e:e + 1], erow[:, e % 2, :], ALU.is_ge, ALU.add))
                nc.vector.tensor_copy(expert[:, :], erow[:, (E - 1) % 2, :]).then_inc(routed, 1)
                dve.wait_ge(routed, 1)

                def rows(k, s):
                    t = bass.ds(2 * k + s, 1)
                    wait(dve, scattered[s], 32 * k)
                    for choice in range(2):
                        ts_(xrows[:, s, choice, 0:D], xs[:, t, :].rearrange("p a d -> p (a d)"), mv_all[:, t, 0],
                            scale[:, t], ALU.subtract, ALU.mult)
                        nc.vector.tensor_copy(xrows[:, s, choice, D:D + 1].bitcast(u32), result_row[:, choice, t])
                    nc.vector.tensor_copy(slot_now[:, s, :].rearrange("p (c a) -> p c a", a=1), slot[:, :, t]).then_inc(rows_ready, 1)
                link(nc.vector.memset(xrows[:, :, :, D:ROW], 0.0))
                rows(0, 0)
                rows(0, 1)
                with dve.Fori(1, TILES // 2, 1) as k:
                    rows(k, 0)
                    rows(k, 1)

                def iteration(k, s, e, nxt, mid, last):
                    j, o = 2 * k + s, 1 - s

                    def hidden(c):
                        dve.wait_ge(silu_ready, 4 * j + c + 1)
                        dve.wait_ge(ab_done, 8 * j + 2 * c + 2)
                        stt(hT[:, s, c, :], ab_ps[c % 2][1][:, :], bias_now[:, s, FC + c:FC + c + 1], sa[:, c % 2, :],
                            ALU.add, ALU.mult).then_inc(h_ready, 1)
                    if mid:
                        wait(dve, y_done, j - 1)
                        hidden(0)
                    if last:
                        dve.wait_ge(next_taken, j)
                        wait(dve, y_scattered[o], 64 * (k if s else k - 1))
                        nc.vector.tensor_copy(result_now[:, o, :], result_next[:, o, :]).then_inc(next_moved, 1)
                    if nxt:
                        dve.wait_ge(xhi_ready, j + 2)
                        tt(xhl[:, o, 1, :], xt_ps[:, :], xhl[:, o, 0, :].bitcast(fp32), ALU.subtract).then_inc(xhl_ready, 1)
                        if last:
                            dve.wait_ge(next_moved, j)
                        nc.vector.tensor_copy(result_next[:, o, :], xg[:, o, :, D].bitcast(u32)).then_inc(next_taken, 1)
                        nc.vector.tensor_copy(bias_now[:, o, :], b1[:, bass.ds(e[2], 1), :]
                                              .rearrange("p a c -> p (a c)")).then_inc(bias_ready, 1)
                    if mid:
                        hidden(1)
                    if nxt:
                        dve.wait_ge(w_hi, j + 2)
                        stt(w1_now[:, o, 1, :, :], w1[:, bass.ds(e[2], 1), :, :].rearrange("p e a f -> p (e a) f"), ln_w[:, 0:1],
                            w1_now[:, o, 0, :, :].bitcast(fp32), ALU.mult, ALU.subtract).then_inc(w_split, 1)
                    if last:
                        dve.wait_ge(y_done, j)
                        tt(ys[:, o, :, :], y_psb[o][:, :].rearrange("p (t d) -> p t d", d=D),
                           b2[:, bass.ds(e[0] * D, D)].unsqueeze(1).to_broadcast([P, 4, D]), ALU.add).then_inc(y_ready, 1)
                    if mid:
                        hidden(2)
                        hidden(3)
                slot_schedule(dve, iteration)

                def mix(k, m):
                    b = 4 * k + m
                    dve.wait_ge(y_loaded[m], 32 * (k + 1))
                    for t in range(NT):
                        tile = bass.ds(NT * b + t, 1)
                        xt = xs[:, tile, :].rearrange("p a d -> p (a d)")
                        stt(yg[:, m, 0, t, :], yg[:, m, 0, t, :], weight[:, 0, tile], xt, ALU.mult, ALU.add).then_inc(half_mixed, 1)
                    for t in range(NT):
                        tile = bass.ds(NT * b + t, 1)
                        xt = xs[:, tile, :].rearrange("p a d -> p (a d)")
                        dve.wait_ge(half_mixed, NT * b + t + 1)
                        stt(xt, yg[:, m, 1, t, :], weight[:, 1, tile], yg[:, m, 0, t, :], ALU.mult, ALU.add).then_inc(mixed, 1)
                with dve.Fori(0, NB // 4, 1) as k:
                    for m in range(4):
                        mix(k, m)

            @block_b.tensor
            def _(pe):
                pe.wait_ge(wb_scaled, 1)
                with pe.Fori(0, NB // 2, 1) as k:
                    for s in range(2):
                        b = 2 * k + s
                        pe.wait_ge(xf_ready, b + 1)
                        for t in range(NT):
                            last_i = nc.tensor.transpose(ab_ps[s][0][:, t * P:(t + 1) * P], xf[:, s, t, :], ident)
                        last_i.then_inc(xfT_ps, 1)
                    for s in range(2):
                        b = 2 * k + s
                        pe.wait_ge(xfT_ready, b + 1)
                        for t in range(NT):
                            last_i = nc.tensor.matmul((lg_ps, xt_ps)[s][:, t * E:(t + 1) * E], xfT[:, s, t * P:(t + 1) * P],
                                                      wg[:, :], start=True, stop=True)
                        last_i.then_inc(lg_done, 1)
                pe.wait_ge(chosen_ready, 1)
                rhs = chosen[:, :, :].rearrange("p t e -> p (t e)")
                nc.tensor.matmul(cum_ps[:, :], before, rhs, start=True, stop=True)
                nc.tensor.matmul(tot_ps[:, :], ones, rhs, start=True, stop=True).then_inc(cum_ready, 1)
                pe.wait_ge(routed, 1)

                def iteration(k, s, e, nxt, mid, last):
                    j, o = 2 * k + s, 1 - s

                    def hidden(c):
                        wait(pe, h_ready, 4 * j + c - 1)
                        for ab in range(2):
                            for m, (xpart, wpart) in enumerate(((0, 0), (0, 1), (1, 0))):
                                last_i = nc.tensor.matmul(ab_ps[c % 2][ab][:, :], w1_now[:, s, wpart, ab, c * P:(c + 1) * P],
                                                          xhl[:, s, xpart, :], start=m == 0, stop=m == 2)
                            last_i.then_inc(ab_done, 1)
                    if mid:
                        pe.wait_ge(w_split, j + 1)
                        pe.wait_ge(xhl_ready, j + 1)
                        hidden(0)
                    if nxt:
                        pe.wait_ge(xg_loaded[o], 16 * (k + 1 + s))
                        for t in range(4):
                            last_i = nc.tensor.transpose(xt_ps[:, t * P:(t + 1) * P], xg[:, o, t, 0:D], ident)
                        last_i.then_inc(xgT_ps, 1)
                    if mid:
                        hidden(1)
                    if last:
                        pe.wait_ge(h_ready, 4 * j)
                        wait(pe, y_ready, j - 2)
                        for t in range(4):
                            for c in range(FC):
                                last_i = nc.tensor.matmul(y_psb[o][:, t * D:(t + 1) * D], hT[:, o, c, t * P:(t + 1) * P],
                                                          w2[:, bass.ds(e[0] * F + c * D, D)], start=c == 0, stop=c == FC - 1)
                        last_i.then_inc(y_done, 1)
                    if mid:
                        hidden(2)
                        hidden(3)
                slot_schedule(pe, iteration)


def bf16_parts(value, np, bf16):
    high = float(np.float32(value).astype(bf16))
    return high, value - high


def layout_constants():
    import math
    import numpy as np
    bf16 = np.dtype("bfloat16")
    P, S, NC, NG, H, E, TILES = 128, 256, 4, 4, 16, 8, 64
    row = np.arange(P) % 32
    f32 = np.zeros((P, 3 + P), np.float32)
    f32[:, 0] = -0.5
    f32[:, 1] = np.where((row >= 20) & (row < 28), -1, 0)
    f32[:, 2] = np.where((row >= 12) & (row < 20), -1, 0)
    f32[:, 3:] = np.eye(P)
    q = np.arange(P)
    causal = np.where(q[None, :] <= q[:, None], 0, -1e30)
    pos = np.zeros((P, S))
    pos[0] = np.arange(S)
    pos[1:3] = 1
    const_q, const_k = np.zeros((2, P, NC, P))
    h = np.arange(1, H + 1, dtype=np.float32)
    slopes = (np.float32(1) / np.power(np.float32(256), h / np.float32(H))).astype(np.float32)
    for c in range(NC):
        for g in range(NG):
            slope = float(slopes[NG * c + g])
            m, e = math.frexp(slope)
            high = math.ldexp(round(m * 4096), e - 12)
            for base, part in ((0, high), (2, slope - high)):
                p0, p1 = bf16_parts(part, np, bf16)
                const_q[1, c, 32 * g + base], const_q[2, c, 32 * g + base] = p0, p1
                const_q[0, c, 32 * g + base + 1] = -1
                const_k[0, c, 32 * g + base] = 1
                const_k[1, c, 32 * g + base + 1], const_k[2, c, 32 * g + base + 1] = p0, p1
            const_k[1, c, 32 * g + 28] = const_k[1, c, 32 * g + 29] = 1
    b16 = np.concatenate([np.eye(P), np.tile(causal, (1, 4)), np.tile(causal.T, (1, 4)), pos,
                          const_q.reshape(P, -1), const_k.reshape(P, -1)], 1).astype(bf16)
    route = np.concatenate([np.tile(E - np.arange(E), (P, 1)), np.tile(4 * P * (np.arange(2 * TILES // 4 + E + 2) - 1.0), (P, 1))],
                           1).astype(np.float32)
    route16 = np.concatenate([q[:, None] < q[None, :], np.ones((P, P))], 1).astype(bf16)
    fill = np.zeros((P, 8, P + 4), np.uint32)
    fill[:, :, P] = 2 * TILES * P + P * np.arange(8) + q[:, None]
    result_rows = (np.arange(2)[None, :, None] * TILES * P + np.arange(TILES)[None, None, :] * P
                   + q[:, None, None]).astype(np.uint32)
    return f32, b16, route, route16, fill.view(np.float32), result_rows


def wide(w, np):
    out = np.zeros((128, 4, 4, 32), w.dtype)
    wt = w.T.reshape(128, 4, 4, 8)
    for copy in range(3):
        out[:, :, :, 4 + 8 * copy:12 + 8 * copy] = wt
    return out.reshape(128, 4, 128)


def kernel(L0_attn_x, L0_attn_W_Q, L0_attn_W_K, L0_attn_W_V, L0_attn_W_O, L0_ffn_ln_w, L0_ffn_Wg, L0_ffn_bg, L0_ffn_W1a,
           L0_ffn_b1a, L0_ffn_W1b, L0_ffn_b1b, L0_ffn_W2, L0_ffn_b2):
    import numpy as np
    import concourse.bacc as bacc
    from concourse.bass_utils import run_bass_kernel_spmd

    f32, b16, route, route16, fill, result_rows = layout_constants()
    E, F, D = L0_ffn_W2.shape
    w2 = np.asarray(L0_ffn_W2).reshape(E, F // 128, 128, D).transpose(2, 0, 1, 3).reshape(128, E * F // 128 * D)
    b1 = np.stack([np.asarray(b).reshape(E, F // 128, 128) for b in (L0_ffn_b1a, L0_ffn_b1b)], 1)
    b1 = b1.transpose(3, 0, 1, 2).reshape(128, E, 2 * F // 128)
    ins = [L0_attn_x, wide(np.asarray(L0_attn_W_Q), np), wide(np.asarray(L0_attn_W_K), np), np.asarray(L0_attn_W_V).T,
           np.asarray(L0_attn_W_O).T, f32, b16, L0_ffn_ln_w, L0_ffn_Wg, L0_ffn_bg, L0_ffn_W1a, b1, L0_ffn_W1b, w2, L0_ffn_b2, route, route16, fill, result_rows]
    nc = bacc.Bacc("TRN2", target_bir_lowering=False, num_devices=1)
    arrays, args = {}, []
    for n, a in enumerate(ins):
        a = np.ascontiguousarray(a)
        arrays[f"in_{n}_dram"] = a
        args.append(nc.dram_tensor(f"in_{n}_dram", a.shape, mybir.dt.from_np(a.dtype), kind="ExternalInput").ap())
    args.append(nc.dram_tensor("out_0_dram", L0_attn_x.shape, mybir.dt.float32, kind="ExternalOutput").ap())
    build_program(nc, *args)
    r = run_bass_kernel_spmd(nc, [arrays], core_ids=[0])
    return r.results[0]["out_0_dram"]
```

```python
import concourse.bass as bass
from concourse import mybir
from contextlib import ExitStack


def build_program(nc, x_in, wq_in, wk_in, wv_in, wo_in, const_f32, const_bf16, ln_w_in, wg_in, bg_in, w1a_in, b1_in,
                  w1b_in, w2_in, b2_in, route_f32, route_bf16, empty_in, result_rows_in, out):
    fp32 = mybir.dt.float32
    fp32r = mybir.dt.float32r
    bf16 = mybir.dt.bfloat16
    i32, u32 = mybir.dt.int32, mybir.dt.uint32
    ALU = mybir.AluOpType
    ACT = mybir.ActivationFunctionType
    AX = mybir.AxisListType

    P = 128
    NB, S, D = x_in.shape
    H, HD = 16, 8
    NT = S // P
    NC, NG = 4, 4
    TILES = NB * NT
    EPS = 1e-5
    RMS_EPS = 2.0 ** -23
    E, _, F = w1a_in.shape
    FC = F // P
    CHUNK = 4 * P
    SLOT_TILES = 2 * TILES * P // CHUNK + E - 1
    REGION = TILES * P // CHUNK + 1
    EMPTY_TILES = SLOT_TILES - 2 * TILES * P // CHUNK
    RT = 2 * NT
    QT = 4
    QUADS = TILES // QT
    ROW = D + 4
    QK_SCALE = float(HD) ** -0.5

    ctx = ExitStack()
    with ctx:
        def sb(name, shape, dt):
            return ctx.enter_context(nc.sbuf_tensor(name, shape, dt))

        def sem(name):
            return ctx.enter_context(nc.semaphore(name))

        xs = sb("xs", [P, TILES, D], fp32)
        cf = sb("cf", [P, 3 + P], fp32)
        minus_half, lo_rows_q, lo_rows_k = cf[:, 0:1], cf[:, 1:2], cf[:, 2:3]
        ident = cf[:, 3:3 + P]
        mv_all = sb("mv_all", [P, TILES, 2], fp32)
        xs_dram = nc.dram_tensor("expert_inputs", [(E * REGION + EMPTY_TILES) * CHUNK, ROW], fp32, kind="Internal").ap()
        ys_dram = nc.dram_tensor("expert_outputs", [2 * TILES * P + (EMPTY_TILES + E) * CHUNK, D], fp32, kind="Internal").ap()
        w1 = sb("w1", [P, E, 2, F], fp32)
        b1 = sb("b1", [P, E, 2 * FC], fp32)
        ln_w = sb("ln_w", [P, 1], fp32)
        rc = sb("rc", [P, 2 * E + SLOT_TILES + 3], fp32)
        preference, region_starts, slot_numbers = rc[:, 0:E], rc[:, E:2 * E], rc[0:1, 2 * E:]
        best = sb("best", [P, 2, TILES], fp32)
        expert = sb("expert", [1, SLOT_TILES + 3], i32)
        slot_tile = sb("slot_tile", [1, SLOT_TILES + 3], i32)
        next_rows = sb("next_rows", [P, E], fp32)
        tables_chain = sem("tables_chain")
        mix_chain = sem("mix_chain")
        routed = sem("routed")
        tails_filled = sem("tails_filled")
        scattered = sem("scattered")
        wb_loaded = sem("wb_loaded")
        experts_loaded = sem("experts_loaded")
        empty_filled = sem("empty_filled")

        def wait(eng, semaphore, value):
            if not isinstance(value, int) or value > 0:
                eng.wait_ge(semaphore, value)

        with ExitStack() as part_a:
            def sba(name, shape, dt):
                return part_a.enter_context(nc.sbuf_tensor(name, shape, dt))

            wq = sba("wq", [P, NC, P], fp32)
            wk = sba("wk", [P, NC, P], fp32)
            wv = sba("wv", [P, D], fp32)
            wo = sba("wo", [P, D], fp32)
            cb = sba("cb", [P, P + 8 * P + S + 2 * NC * P], bf16)
            causalT = cb[:, 5 * P:9 * P]
            ident_bf = cb[:, 0:P]
            causal = cb[:, P:5 * P]
            pos_rows = cb[:, 9 * P:9 * P + S]
            const_q = cb[:, 9 * P + S:9 * P + S + NC * P].rearrange("p (c m) -> p c m", c=NC)
            const_k = cb[:, 9 * P + S + NC * P:].rearrange("p (c m) -> p c m", c=NC)

            stats = sba("stats", [P, NT, 6], fp32)
            mean_var = sba("mean_var", [P, NT, 2], fp32)
            var_eps = sba("var_eps", [P, NT], fp32)
            rstd = sba("rstd", [P, NT], fp32)
            xn = sba("xn", [P, NT, D], fp32)
            xnT = sba("xnT", [P, 2, S], fp32)
            hi = sba("hi", [P, 2, 2, S], fp32r)
            qs = sba("qs", [P, NC, S], fp32r)
            ks = sba("ks", [P, 2, NC, S], fp32r)
            qm = [sba(f"qm{i}", [P, NC, NG, S], fp32r) for i in range(2)]
            km = sba("km", [P, NC, NG, S], fp32r)
            va = sba("va", [P, 2, NT, H, 32], fp32)
            negmax = sba("negmax", [P, NT, 2, NG], fp32)
            parts = sba("parts", [P, NT, NG, 2, 2], fp32r)
            maxT = sba("maxT", [4 * NG, 2, S], fp32r)
            pk0 = sba("pk0", [P, 2, NG, S], fp32)
            pk1 = sba("pk1", [P, 2, 2, NG, P], fp32)
            oT = sba("oT", [P, 2, NC, S], fp32)
            rden = sba("rden", [P, NT, H], fp32)
            on = sba("on", [P, NT, H, HD], fp32)
            onT = sba("onT", [P, S], fp32)

            count = sba("count", [P, E], fp32)
            icount = sba("icount", [P, 2, E], i32)
            tiles = sba("tiles", [P, E], fp32)
            ends = sba("ends", [P, 4, E], fp32)
            skip = sba("skip", [P, E], fp32)
            past = sba("past", [1, SLOT_TILES + 3, E], fp32)
            skips = sba("skips", [1, SLOT_TILES + 3, E], fp32)
            expert_f = sba("expert_f", [1, SLOT_TILES + 3], fp32)
            tile_f = sba("tile_f", [1, 2, SLOT_TILES + 3], fp32)
            tail_row = sba("tail_row", [1, E], i32)
            last_slots = [sba(f"last_slots{i}", [P, 2, RT], u32) for i in range(2)]
            wg = sba("wg", [P, E], fp32)
            bg = sba("bg", [P, E], fp32)
            rb = sba("rb", [P, 2 * P], bf16)
            before, ones = rb[:, 0:P], rb[:, P:2 * P]
            result_row = sba("result_row", [P, TILES, 2], u32)
            xrows = sba("xrows", [P, RT, 2, ROW], fp32)
            xfT = sba("xfT", [P, RT * P], fp32)
            logits = sba("logits", [P, RT, E], fp32)
            rest = sba("rest", [P, RT, E], fp32)
            marks = sba("marks", [P, RT, E], fp32)
            first = sba("first", [P, 2, RT], fp32)
            foremost = sba("foremost", [P, 2, RT], fp32)
            top = sba("top", [P, 2, RT, E], fp32)
            chosen = sba("chosen", [P, RT, E], bf16)
            place = sba("place", [P, RT, E], fp32)
            places = sba("places", [P, 2, RT, E], fp32)
            slot = sba("slot", [P, 2, RT], fp32)
            slot_now = sba("slot_now", [P, 2, RT], u32)
            dev = [sba(f"dev{i}", [P, RT], fp32) for i in range(6)]
            var_now = sba("var_now", [P, RT], fp32)
            scale = sba("scale", [P, RT], fp32)
            wb_scaled = sem("wb_scaled")
            mv_saved = sem("mv_saved")
            dev_chain = sem("dev_chain")
            scale_ready = sem("scale_ready")
            xf_ready = sem("xf_ready")
            xfT_ps = sem("xfT_ps")
            xfT_ready = sem("xfT_ready")
            lg_done = sem("lg_done")
            lg_taken = sem("lg_taken")
            picked = sem("picked")
            place_ps = sem("place_ps")
            place_taken = sem("place_taken")
            chain_c = sem("chain_c")
            slots_ready = sem("slots_ready")
            mv1 = sba("mv1", [P, NT, 2], fp32)
            stats1 = sba("stats1", [P, NT, 6], fp32)
            bn1 = sem("bn1")
            mv1_ready = sem("mv1_ready")
            turn_a = sem("turn_a")
            turn_p = sem("turn_p")
            s1 = part_a.enter_context(nc.psum_tensor("s1", [P, 2, 512], fp32))
            s2 = part_a.enter_context(nc.psum_tensor("s2", [P, 2, 512], fp32))
            X = [part_a.enter_context(nc.psum_tensor(f"x{i}", [P, 512], fp32)) for i in range(4)]

            x_loaded = sem("x_loaded")
            rest_loaded = sem("rest_loaded")
            w_loaded = sem("w_loaded")
            wq_scaled = sem("wq_scaled")
            zeroed = sem("zeroed")
            bn = sem("bn")
            stats_ready = sem("stats_ready")
            var_ready = sem("var_ready")
            rstd_ready = sem("rstd_ready")
            xn_ready = sem("xn_ready")
            xnT_ps = sem("xnT_ps")
            xnT_ready = sem("xnT_ready")
            km_ready = sem("km_ready")
            qm_ready = sem("qm_ready")
            v_ps = sem("v_ps")
            v_ready = sem("v_ready")
            hi_k = sem("hi_k")
            hi_q = sem("hi_q")
            proj_k = sem("proj_k")
            proj_q = sem("proj_q")
            stack_k = sem("stack_k")
            stack_q = sem("stack_q")
            split_done = sem("split_done")
            s1_ps = sem("s1_ps")
            max_ready = sem("max_ready")
            maxT_ps = sem("maxT_ps")
            max_hi = sem("max_hi")
            maxT_ready = sem("maxT_ready")
            max_placed = [sem(f"max_placed{p}") for p in range(2)]
            s2_ps = sem("s2_ps")
            exp_ready = sem("exp_ready")
            pv_ps = sem("pv_ps")
            oT_ready = sem("oT_ready")
            oq_ps = sem("oq_ps")
            rden_ready = sem("rden_ready")
            on_ready = sem("on_ready")
            onT_ps = sem("onT_ps")
            onT_ready = sem("onT_ready")
            y_ps = sem("y_ps")
            x1_ready = sem("x1_ready")

            FIRST, LAST = -2, NB + 4
            STEADY = 6
            HALVES = 2 * NB

            def schedule(eng, iteration):
                def step(i):
                    for h in range(2):
                        iteration(i, h, even=i % 2 == 0)
                for i in range(FIRST, STEADY):
                    step(i)
                with eng.Fori(STEADY, NB - 4, 2) as i:
                    for h in range(2):
                        iteration(i, h, even=True)
                    for h in range(2):
                        iteration(i + 1, h, even=False)
                for i in range(NB - 4, LAST):
                    step(i)

            def within(n):
                return not isinstance(n, int) or 0 <= n < NB

            def cap(value, limit):
                return min(value, limit) if isinstance(value, int) else value

            def as_rows(buffer):
                return buffer[:, 0:RT * 2 * ROW].rearrange("p (t a r) -> p t a r", t=RT, a=2)
            last_rows = (as_rows(pk0[:, :, :, :].rearrange("p c g s -> p (c g s)")),
                         as_rows(pk1[:, :, :, :, :].rearrange("p a c g s -> p (a c g s)")))

            def rows_and_slots(i):
                if isinstance(i, int) and i >= NB:
                    return last_rows[(i - NB) // 2], last_slots[(i - NB) // 2]
                return xrows, slot_now

            def picks_at(i, even):
                return even and (not isinstance(i, int) or 4 <= i < LAST)

            def sends_at(i, even):
                return not even and (not isinstance(i, int) or 5 <= i < LAST)

            def pair_of(i, h):
                return i + 1 + h, 1 - h, 2 * i + 3 + h

            block = part_a.enter_context(nc.Block())

            @block.sync
            def _(sp):
                def load_x(first_batch, batches, loaded):
                    sp.dma_start(xs[:, NT * first_batch:NT * (first_batch + batches), :],
                                 x_in[first_batch:first_batch + batches].rearrange("b (t p) d -> p (b t) d", p=P)
                                 ).then_inc(loaded, 16)
                load_x(0, 2, x_loaded)
                sp.dma_start(cf[:, :], const_f32).then_inc(w_loaded, 16)
                sp.dma_start(cb[:, :], const_bf16).then_inc(w_loaded, 16)
                sp.dma_start(wq[:, :, :], wq_in).then_inc(w_loaded, 16)
                sp.dma_start(wk[:, :, :], wk_in).then_inc(w_loaded, 16)
                sp.dma_start(wv[:, :], wv_in).then_inc(w_loaded, 16)
                sp.dma_start(wo[:, :], wo_in).then_inc(w_loaded, 16)
                sp.dma_start(rc[:, :], route_f32).then_inc(wb_loaded, 16)
                sp.dma_start(result_row[:, :, :], result_rows_in).then_inc(wb_loaded, 16)
                sp.dma_start(rb[:, :], route_bf16).then_inc(wb_loaded, 16)
                sp.dma_start(wg[:, :], wg_in).then_inc(wb_loaded, 16)
                sp.dma_start(ln_w[:, :], ln_w_in.rearrange("(p a) -> p a", a=1)).then_inc(wb_loaded, 16)
                sp.dma_start(bg[:, :], bg_in.rearrange("(a e) -> a e", a=1).to_broadcast([P, E])).then_inc(wb_loaded, 16)
                load_x(2, NB - 2, rest_loaded)
                for ab, src in enumerate((w1a_in, w1b_in)):
                    sp.dma_start(w1[:, :, ab, :], src.rearrange("e p f -> p e f")).then_inc(experts_loaded, 16)
                sp.dma_start(b1[:, :, :], b1_in).then_inc(experts_loaded, 16)
                sp.dma_start(xs_dram[E * REGION * CHUNK:, :], empty_in[E * CHUNK:, :]).then_inc(empty_filled, 16)

                def iteration(i, h, even):
                    n, p = i + h, 1 - h
                    if within(n):
                        g = 2 * i + 1 + h
                        buf = (0 if even else 1) if h == 0 else (1 if even else 0)
                        sp.wait_ge(qm_ready, g + 1)
                        sp.wait_ge(maxT_ready, g + 1)
                        for head in range(NG):
                            row = 32 * head + 28
                            sp.dma_start(qm[buf][row:row + 2, 2 * p:2 * p + 2, head, :].bitcast(fp32),
                                         maxT[4 * head:4 * head + 4, p, :].bitcast(fp32)
                                         ).then_inc(max_placed[p], 16)
                schedule(sp, iteration)

                sp.wait_ge(routed, 1)
                tails = nc.values_load_multi_w_load_instructions(tail_row[0:1, :], [sp.engine], min_val=0,
                                                                 max_val=E * REGION * CHUNK - CHUNK)[1]
                for e in range(E):
                    sp.dma_start(xs_dram[bass.ds(tails[e], CHUNK), :],
                                 empty_in[e * CHUNK:(e + 1) * CHUNK, :]).then_inc(tails_filled, 16)

            @block.gpsimd
            def _(pool):
                def zero(buf):
                    return nc.gpsimd.memset(buf.bitcast(fp32), 0.0)

                def inverse_deviation(n):
                    pool.wait_ge(stats_ready, n + 1)
                    pool.sem_inc(turn_p, 1)
                    nc.gpsimd.tensor_scalar(var_eps[:, :], mean_var[:, :, 1], 1.0, EPS, ALU.mult,
                                            ALU.add).then_inc(var_ready, 1)
                    pool.wait_ge(var_ready, n + 1)
                    nc.gpsimd.tensor_tensor(rstd[:, :], var_eps[:, :], minus_half.to_broadcast([P, NT]),
                                            ALU.pow).then_inc(rstd_ready, 1)

                def masked_queries(i, h, even):
                    g = 2 * i + 2 + h
                    buf = 1 if even else 0
                    pool.wait_ge(stack_q, g + 1)
                    wait(pool, s2_ps, 6 * (g - 3))
                    pool.wait_ge(rstd_ready, cap(i + 3, NB))
                    if picks_at(i, even):
                        if h == 0:
                            pool.wait_ge(scale_ready, i - 2)
                            wait(pool, scattered, 64 * (i - 5))
                        else:
                            wait(pool, scattered, 64 * (i - 4))
                    pool.sem_inc(turn_p, 1)
                    for head in range(NG):
                        last = nc.gpsimd.tensor_scalar(qm[buf][32 * head:32 * head + 32, 2 * h:2 * h + 2, head, :],
                                                       qs[32 * head:32 * head + 32, 2 * h:2 * h + 2, :].bitcast(fp32), 1.0,
                                                       0.0, ALU.mult, ALU.add)
                    last.then_inc(qm_ready, 1)

                def scale_group(i):
                    links = [0]

                    def link(instruction):
                        links[0] += 1
                        instruction.then_inc(dev_chain, 2)
                        pool.wait_ge(dev_chain, 6 * (i - 4) + 2 * links[0])
                    tt = nc.gpsimd.tensor_tensor
                    half = minus_half.to_broadcast([P, RT])
                    pool.wait_ge(mv_saved, i - 2)
                    wait(pool, xf_ready, i - 4)
                    pool.sem_inc(turn_p, 1)
                    link(nc.gpsimd.tensor_scalar(dev[0][:, :], var_now[:, :], 1.0, EPS, ALU.mult, ALU.add))
                    link(tt(dev[1][:, :], dev[0][:, :], half, ALU.pow))
                    link(tt(dev[2][:, :], dev[1][:, :], dev[1][:, :], ALU.mult))
                    link(tt(dev[3][:, :], dev[2][:, :], var_now[:, :], ALU.mult))
                    pool.sem_inc(turn_p, 1)
                    link(nc.gpsimd.tensor_scalar(dev[4][:, :], dev[3][:, :], 1.0, RMS_EPS, ALU.mult, ALU.add))
                    link(tt(dev[5][:, :], dev[4][:, :], half, ALU.pow))
                    assert links[0] == 6
                    tt(scale[:, :], dev[1][:, :], dev[5][:, :], ALU.mult).then_inc(scale_ready, 2)

                def send_rows(i, h):
                    rows, slots = rows_and_slots(i)
                    pool.wait_ge(slots_ready, i - 3)
                    pool.sem_inc(turn_p, 1)
                    for t in range(2 * h, 2 * h + 2):
                        for choice in range(2):
                            nc.gpsimd.indirect_dma_start(
                                xs_dram, bass.IndirectOffsetOnAxis(slots[:, choice, t:t + 1], 0),
                                rows[:, t, choice, :], None).then_inc(scattered, 16)

                def iteration(i, h, even):
                    if within(i + 1):
                        masked_queries(i, h, even)
                    wait(pool, qm_ready, cap(2 * i + 3 + h, HALVES))
                    if h == 1 and (not isinstance(i, int) or i + 3 < NB):
                        inverse_deviation(i + 3)
                    if h == 1 and not even and (not isinstance(i, int) or 3 <= i < LAST - 1):
                        scale_group(i + 1)
                    if h == 1 and sends_at(i, even):
                        send_rows(i, 0)
                        if isinstance(i, int) and i == LAST - 1:
                            send_rows(i, 1)
                    if h == 0 and even and (not isinstance(i, int) or 6 <= i):
                        send_rows(i - 1, 1)
                zero(qm[0][:, :, :, :])
                zero(qm[1][:, :, :, :])
                pool.wait_ge(w_loaded, 96)
                inverse_deviation(0)
                nc.gpsimd.memset(va[:, :, :, :, :].rearrange("p a t h e -> p (a t h e)"), 0.0).then_inc(zeroed, 1)
                pool.wait_ge(zeroed, 1)
                nc.gpsimd.memset(va[:, :, :, :, HD:HD + 1], 1.0).then_inc(zeroed, 1)
                schedule(pool, iteration)

            @block.scalar
            def _(act):
                def take_values(i, par):
                    if within(i + 1):
                        act.wait_ge(v_ps, i + 2)
                        nc.scalar.copy(va[:, 1 - par, :, :, 0:HD],
                                       X[3][:, S:2 * S].rearrange("p (t h d) -> p t h d", t=NT, h=H)).then_inc(v_ready, 1)

                def iteration(i, h, even):
                    par = 0 if even else 1
                    n_p, p_p, g_p = pair_of(i, h)
                    n_m, g_m = i + h, 2 * i + 1 + h
                    if within(n_m):
                        act.wait_ge(maxT_ps, g_m + 1)
                        wait(act, max_placed[1 - h], 64 * n_m)
                        nc.scalar.copy(maxT[:, 1 - h, :], X[2][0:4 * NG, 0:S]).then_inc(maxT_ready, 1)
                    if within(n_p):
                        act.wait_ge(proj_k, g_p + 1)
                        wait(act, stack_k, g_p)
                        nc.scalar.copy(hi[:, 0, :, :].rearrange("p c s -> p (c s)"), X[1][:, :]).then_inc(hi_k, 1)
                    n_v, g_v = i - 1 + h, 2 * i - 1 + h
                    if within(n_v):
                        act.wait_ge(pv_ps, 2 * g_v + 2)
                        wait(act, oq_ps, 2 * (i - 2 + h))
                        nc.scalar.copy(oT[:, par if h else 1 - par, 2 * (1 - h):2 * (1 - h) + 2, :].rearrange("p c s -> p (c s)"),
                                       X[0][:, :]).then_inc(oT_ready, 1)
                    g = 2 * i + h
                    if within(i):
                        wait(act, pv_ps, 2 * g - 2)
                        for b in range(2):
                            act.wait_ge(s2_ps, 6 * g + b + 1)
                            nc.scalar.activation(pk1[:, h, b, :, :].rearrange("p g q -> p (g q)"), s2[:, b, :],
                                                 ACT.Exp).then_inc(exp_ready, 1)
                    if h == 0 and within(i - 2):
                        act.wait_ge(onT_ps, i - 1)
                        nc.scalar.copy(onT[:, :], X[3][:, 0:S]).then_inc(onT_ready, 1)
                    if h == 1 and even:
                        take_values(i, par)
                    if within(n_p):
                        act.wait_ge(proj_q, g_p + 1)
                        wait(act, stack_q, g_p)
                        nc.scalar.copy(hi[:, 1, :, :].rearrange("p c s -> p (c s)"), X[2][:, :]).then_inc(hi_q, 1)
                    for u in (1, 2):
                        if within(i):
                            wait(act, pv_ps, 2 * g - 2 + u)
                            for b in range(2):
                                act.wait_ge(s2_ps, 6 * g + 2 * u + b + 1)
                                nc.scalar.activation(pk0[:, u - 1, 2 * b:2 * b + 2, :].rearrange("p h q -> p (h q)"),
                                                     s2[:, b, :], ACT.Exp).then_inc(exp_ready, 1)
                    if h == 1 and not even:
                        take_values(i, par)
                    if h == 0 and within(i + 2):
                        act.wait_ge(xnT_ps, i + 3)
                        wait(act, v_ps, i + 1)
                        nc.scalar.copy(xnT[:, par, :], X[3][:, 0:S]).then_inc(xnT_ready, 1)
                    if h == 1 and picks_at(i, even):
                        act.wait_ge(xfT_ps, i - 2)
                        nc.scalar.copy(xfT[:, :], X[3][:, :]).then_inc(xfT_ready, 2)
                schedule(act, iteration)

            @block.vector
            def _(dve):
                tt, ts_, stt = nc.vector.tensor_tensor, nc.vector.tensor_scalar, nc.vector.scalar_tensor_tensor
                reduce = nc.vector.tensor_reduce

                def layer_stats(n):
                    for t in range(NT):
                        nc.vector.bn_stats(stats[:, t, :], xs[:, NT * n + t, :]).then_inc(bn, 1)
                    dve.wait_ge(bn, 2 * n + 2)
                    dve.sem_inc(turn_a, 1)
                    for t in range(NT):
                        last = nc.vector.bn_aggr(mean_var[:, t, :], stats[:, t, :])
                    last.then_inc(stats_ready, 1)

                def normalise(n):
                    dve.wait_ge(rstd_ready, n + 1)
                    wait(dve, xnT_ps, n)
                    for t in range(NT):
                        last = ts_(xn[:, t, :], xs[:, NT * n + t, :], mean_var[:, t, 0:1], rstd[:, t:t + 1], ALU.subtract,
                                   ALU.mult)
                    last.then_inc(xn_ready, 1)

                def stack(q, buf, par, p, g):
                    dve.wait_ge(hi_q if q else hi_k, g + 1)
                    if q:
                        wait(dve, s1_ps, 6 * (g - 1))
                        wait(dve, qm_ready, g - 1)
                    else:
                        wait(dve, s2_ps, 6 * (g - 3))
                    dst = qs[:, 2 * p:2 * p + 2, :] if q else ks[:, par, 2 * p:2 * p + 2, :]
                    stt(dst, hi[:, q, :, :].bitcast(fp32), lo_rows_q if q else lo_rows_k,
                        X[1 + q][:, :].rearrange("p (c s) -> p c s", c=2), ALU.mult,
                        ALU.add).then_inc(stack_q if q else stack_k, 1)

                def masked_keys(par, p, g):
                    dve.wait_ge(stack_k, g + 1)
                    wait(dve, s1_ps, 6 * (g - 1))
                    for head in range(NG):
                        last = nc.vector.tensor_copy(km[32 * head:32 * head + 32, 2 * p:2 * p + 2, head, :],
                                                     ks[32 * head:32 * head + 32, par, 2 * p:2 * p + 2, :])
                    last.then_inc(km_ready, 1)

                def maxima(g, u):
                    if u == 0:
                        wait(dve, split_done, g)
                    for b in range(2):
                        dve.wait_ge(s1_ps, 6 * g + 2 * u + b + 1)
                        if u == 0:
                            src = s1[:, b, :].rearrange("p (g k) -> p g k", k=P)
                            dst = negmax[:, 0, b, :]
                        else:
                            src = s1[:, b, :].rearrange("p (g k) -> p g k", k=S)
                            dst = negmax[:, 1, u - 1, 2 * b:2 * b + 2]
                        reduce(dst, src, AX.X, ALU.max, negate=True).then_inc(max_ready, 1)

                def split_maxima(g):
                    dve.wait_ge(max_ready, 6 * g + 6)
                    wait(dve, maxT_ps, g)
                    by_head = negmax[:, :, :, :].rearrange("p t c g -> p t g c")
                    nc.vector.tensor_copy(parts[:, :, :, 0, :], by_head).then_inc(max_hi, 1)
                    dve.wait_ge(max_hi, g + 1)
                    tt(parts[:, :, :, 1, :], by_head, parts[:, :, :, 0, :].bitcast(fp32),
                       ALU.subtract).then_inc(split_done, 1)

                def weighted_values(i, t):
                    dve.wait_ge(oq_ps, 2 * i - 1 + t)
                    wait(dve, onT_ps, i - 1)
                    o = X[1][:, :].rearrange("p (h e) -> p h e", h=H)
                    nc.vector.reciprocal(rden[:, t, :], o[:, :, HD]).then_inc(rden_ready, 1)
                    dve.wait_ge(rden_ready, 2 * i - 1 + t)
                    tt(on[:, t, :, :], o[:, :, 0:HD], rden[:, t, :].unsqueeze(2).to_broadcast([P, H, HD]),
                       ALU.mult).then_inc(on_ready, 1)

                def add_attention(i):
                    dve.wait_ge(y_ps, i - 1)
                    xt = xs[:, bass.ds(NT * (i - 2), NT), :]
                    tt(xt, X[3][:, S:2 * S].rearrange("p (t d) -> p t d", t=NT), xt, ALU.add).then_inc(x1_ready, 1)
                    dve.wait_ge(x1_ready, i - 1)
                    dve.sem_inc(turn_a, 1)
                    for t in range(NT):
                        nc.vector.bn_stats(stats1[:, t, :], xs[:, bass.ds(NT * (i - 2) + t, 1), :]
                                           .rearrange("p a d -> p (a d)")).then_inc(bn1, 1)
                    dve.wait_ge(bn1, 2 * (i - 1))
                    wait(dve, mv_saved, i - 2)
                    dve.sem_inc(turn_a, 1)
                    for t in range(NT):
                        last = nc.vector.bn_aggr(mv1[:, t, :], stats1[:, t, :])
                    last.then_inc(mv1_ready, 1)

                def save_statistics(i, even):
                    dve.wait_ge(mv1_ready, i - 1)
                    nc.vector.tensor_copy(mv_all[:, bass.ds(NT * (i - 2), NT), :], mv1[:, :, :])
                    if even:
                        wait(dve, scale_ready, i - 2)
                    start = 0 if even else NT
                    nc.vector.tensor_copy(var_now[:, start:start + NT], mv1[:, :, 1]).then_inc(mv_saved, 1)

                def scaled_rows(i):
                    rows, _ = rows_and_slots(i)
                    dve.wait_ge(scale_ready, i - 2)
                    if rows is xrows:
                        wait(dve, scattered, 64 * (i - 4))
                    dve.sem_inc(turn_a, 1)
                    for t in range(RT):
                        tile = bass.ds(2 * i - 8 + t, 1)
                        last = ts_(rows[:, t, 0, 0:D], xs[:, tile, :].rearrange("p a d -> p (a d)"),
                                   mv_all[:, tile, 0], scale[:, t:t + 1], ALU.subtract, ALU.mult)
                    last.then_inc(xf_ready, 2)
                    nc.vector.tensor_copy(rows[:, :, :, D].bitcast(u32), result_row[:, bass.ds(2 * i - 8, RT), :])
                    dve.wait_ge(xf_ready, i - 2)
                    nc.vector.tensor_copy(rows[:, :, 1, 0:D], rows[:, :, 0, 0:D])

                def take_logits(group2):
                    dve.wait_ge(lg_done, group2 + 2)
                    tt(logits[:, :, :], X[3][:, 0:RT * E].rearrange("p (t e) -> p t e", t=RT),
                       bg[:, :].unsqueeze(1).to_broadcast([P, RT, E]), ALU.add).then_inc(lg_taken, 2)

                def pick_step(m, group2):
                    choice, r = divmod(m, 6)
                    if m == 0:
                        dve.wait_ge(lg_taken, group2 + 2)
                    else:
                        dve.wait_ge(picked, 12 * group2 + 2 * m)

                    def over_e(v):
                        return v.unsqueeze(2).to_broadcast([P, RT, E])
                    pref = preference.unsqueeze(1).to_broadcast([P, RT, E])
                    lg = rest if choice else logits
                    if r == 0:
                        done = reduce(first[:, choice, :], lg[:, :, :], AX.X, ALU.max)
                    elif r == 1:
                        nc.vector.tensor_copy(best[:, choice, bass.ds(2 * group2, RT)], first[:, choice, :])
                        done = tt(marks[:, :, :], lg[:, :, :], over_e(first[:, choice, :]), ALU.is_equal)
                    elif r == 2:
                        done = tt(marks[:, :, :], marks[:, :, :], pref, ALU.mult)
                    elif r == 3:
                        done = reduce(foremost[:, choice, :], marks[:, :, :], AX.X, ALU.max)
                    elif r == 4:
                        done = tt(top[:, choice, :, :], pref, over_e(foremost[:, choice, :]), ALU.is_equal)
                    elif choice == 0:
                        done = stt(rest[:, :, :], top[:, 0, :, :], -3e38, lg[:, :, :], ALU.mult, ALU.add)
                    else:
                        done = tt(chosen[:, :, :], top[:, 0, :, :], top[:, 1, :, :], ALU.add)
                    done.then_inc(picked, 2)

                def places_of_rows(i):
                    links = [0]

                    def link(instruction):
                        links[0] += 1
                        instruction.then_inc(chain_c, 2)
                        dve.wait_ge(chain_c, 5 * (i - 5) + 2 * links[0])
                    dve.wait_ge(place_ps, i - 3)
                    link(tt(place[:, :, :], X[3][:, 0:RT * E].rearrange("p (t e) -> p t e", t=RT),
                            next_rows[:, :].unsqueeze(1).to_broadcast([P, RT, E]), ALU.add))
                    link(tt(next_rows[:, :], X[3][:, RT * E:RT * E + E], next_rows[:, :], ALU.add))
                    dve.sem_inc(place_taken, 2)
                    link(tt(places[:, :, :, :], top[:, :, :, :],
                            place[:, :, :].unsqueeze(1).to_broadcast([P, 2, RT, E]), ALU.mult))
                    link(reduce(slot[:, :, :], places[:, :, :, :], AX.X, ALU.add))
                    link(nc.vector.tensor_copy(rows_and_slots(i)[1][:, :, :], slot[:, :, :]))
                    assert links[0] == 5
                    dve.sem_inc(slots_ready, 2)

                nc.vector.memset(xrows[:, :, :, D:ROW], 0.0)
                nc.vector.memset(km[:, :, :, :].bitcast(fp32), 0.0)
                dve.wait_ge(x_loaded, 16)
                layer_stats(0)
                dve.wait_ge(w_loaded, 96)
                ts_(wq[:, :, :], wq[:, :, :], QK_SCALE, None, ALU.mult).then_inc(wq_scaled, 1)
                dve.wait_ge(wb_loaded, 96)
                ts_(wg[:, :], wg[:, :], ln_w[:, 0:1], None, ALU.mult).then_inc(wb_scaled, 1)
                nc.vector.tensor_copy(next_rows[:, :], region_starts)

                def iteration(i, h, even):
                    par = 0 if even else 1
                    n_p, p_p, g_p = pair_of(i, h)
                    par_p = 1 - par if h == 0 else par
                    g = 2 * i + 2 + h
                    if isinstance(i, int) and i == -1 and h == 1:
                        dve.wait_ge(rest_loaded, 16)
                    def pick(*steps):
                        if h == 0 and sends_at(i, even):
                            for m in steps:
                                pick_step(m, i - 5)
                    pick(0)
                    if within(i + 1):
                        maxima(g, 0)
                    pick(1)
                    if within(n_p):
                        stack(0, 0, par_p, p_p, g_p)
                    pick(2)
                    if h == 1:
                        if within(i - 2):
                            save_statistics(i, even)
                        if not isinstance(i, int) or i + 3 < NB:
                            layer_stats(i + 3)
                    if h == 0 and within(i + 2):
                        normalise(i + 2)
                    pick(3)
                    if within(i + 1):
                        maxima(g, 1)
                    if h == 1 and sends_at(i, even):
                        places_of_rows(i)
                    if h == 1 and picks_at(i, even):
                        scaled_rows(i)
                    pick(4)
                    if within(n_p):
                        masked_keys(par_p, p_p, g_p)
                        pick(5)
                        stack(1, 1, 0, p_p, g_p)
                        pick(6)
                    else:
                        pick(5, 6)
                    if h == 0 and within(i - 2):
                        add_attention(i)
                    pick(7)
                    if within(i + 1):
                        maxima(g, 2)
                        pick(8)
                        split_maxima(g)
                    else:
                        pick(8)
                    pick(9)
                    if within(i - 1):
                        weighted_values(i, h)
                    pick(10, 11)
                    if h == 1 and picks_at(i, even):
                        take_logits(i - 4)
                schedule(dve, iteration)

                links = [0]

                def link(instruction):
                    links[0] += 1
                    instruction.then_inc(tables_chain, 1)
                    dve.wait_ge(tables_chain, links[0])

                link(tt(count[:, :], next_rows[:, :], region_starts, ALU.subtract))
                link(ts_(count[:, :], count[:, :], float(CHUNK - 1), None, ALU.add))
                link(nc.vector.tensor_copy(icount[:, 0, :], count[:, :]))
                link(ts_(icount[:, 1, :], icount[:, 0, :], CHUNK.bit_length() - 1, None, ALU.logical_shift_right))
                link(nc.vector.tensor_copy(tiles[:, :], icount[:, 1, :]))
                link(ts_(skip[:, :], tiles[:, :], -1.0, float(REGION), ALU.mult, ALU.add))
                link(nc.vector.tensor_copy(ends[:, 0, :], tiles[:, :]))
                for m, step in enumerate((1, 2, 4)):
                    nc.vector.tensor_copy(ends[:, m + 1, 0:step], ends[:, m, 0:step])
                    link(tt(ends[:, m + 1, step:E], ends[:, m, step:E], ends[:, m, 0:E - step], ALU.add))
                n_ = SLOT_TILES + 3
                numbers = slot_numbers.unsqueeze(2).to_broadcast([1, n_, E])
                link(tt(past[:, :, :], numbers, ends[0:1, 3, :].unsqueeze(1).to_broadcast([1, n_, E]), ALU.is_ge))
                link(nc.vector.tensor_reduce(expert_f[:, :], past[:, :, 0:E - 1], AX.X, ALU.add))
                link(nc.vector.tensor_copy(expert[:, :], expert_f[:, :]))
                link(tt(skips[:, :, :], past[:, :, :], skip[0:1, :].unsqueeze(1).to_broadcast([1, n_, E]), ALU.mult))
                link(nc.vector.tensor_reduce(tile_f[:, 0, :], skips[:, :, :], AX.X, ALU.add))
                link(tt(tile_f[:, 1, :], tile_f[:, 0, :], slot_numbers, ALU.add))
                link(nc.vector.tensor_copy(slot_tile[:, :], tile_f[:, 1, :]))
                nc.vector.tensor_copy(tail_row[:, :], next_rows[0:1, :]).then_inc(routed, 1)

            @block.tensor
            def _(pe):
                pe.wait_ge(w_loaded, 96)
                pe.wait_ge(wq_scaled, 1)
                pe.wait_ge(wb_scaled, 1)

                def project(q, par, p):
                    w, const = ((wk, const_k), (wq, const_q))[q]
                    for c in range(2):
                        ch = 2 * p + c
                        dst = X[1 + q][:, c * S:(c + 1) * S]
                        nc.tensor.matmul(dst, const[:, ch, :], pos_rows, start=True, stop=False)
                        last = nc.tensor.matmul(dst, w[:, ch, :], xnT[:, par, :], start=False, stop=True)
                    last.then_inc(proj_q if q else proj_k, 1)

                def scores_for_max(g, p, u):
                    if u == 0:
                        pe.wait_ge(km_ready, g + 1)
                        pe.wait_ge(stack_q, g + 1)
                    for b in range(2):
                        wait(pe, max_ready, 6 * g + 2 * u + b - 1)
                        if u == 0:
                            c = 2 * p + b
                            nc.tensor.matmul(s1[:, b, :], qs[:, c, 0:P], km[:, c, :, 0:P], start=True, stop=False)
                            last = nc.tensor.matmul(s1[:, b, :], ident_bf, causal, start=False, stop=True)
                        else:
                            c = 2 * p + u - 1
                            nc.tensor.matmul(s1[:, b, :], qs[:, c, P:S], km[:, c, 2 * b:2 * b + 2, :], start=True, stop=False)
                            diag = s1[:, b, :].rearrange("p (g k) -> p g k", g=2)[:, :, P:S]
                            last = nc.tensor.matmul(diag, ident_bf, causal[:, 0:2 * P], start=False, stop=True)
                        last.then_inc(s1_ps, 1)

                def scores_for_exp(i, g, p, par, u):
                    if u == 0:
                        pe.wait_ge(max_placed[p], 64 * (i + 1))
                    for b in range(2):
                        wait(pe, exp_ready, 6 * g + 2 * u + b - 1)
                        if u == 0:
                            c = 2 * p + b
                            nc.tensor.matmul(s2[:, b, :], ks[:, par, c, P:S], qm[par][:, c, :, P:S], start=True, stop=False)
                            last = nc.tensor.matmul(s2[:, b, :], ident_bf, causalT, start=False, stop=True)
                        else:
                            c = 2 * p + u - 1
                            nc.tensor.matmul(s2[:, b, :], ks[:, par, c, 0:P], qm[par][:, c, 2 * b:2 * b + 2, :],
                                             start=True, stop=False)
                            diag = s2[:, b, :].rearrange("p (g q) -> p g q", g=2)[:, :, 0:P]
                            last = nc.tensor.matmul(diag, ident_bf, causalT[:, 0:2 * P], start=False, stop=True)
                        last.then_inc(s2_ps, 1)

                def weigh_values(g, p, par, c):
                    pe.wait_ge(exp_ready, 2 * (3 * g + 2 + c))
                    if c == 0:
                        wait(pe, oT_ready, g)
                    first_head = NG * (2 * p + c)
                    for head in range(NG):
                        nc.tensor.matmul(X[0][32 * head:32 * head + 32, c * S:(c + 1) * S], va[:, par, 0, first_head + head, :],
                                         pk0[:, c, head, :], start=True, stop=False)
                    for head in range(NG):
                        last = nc.tensor.matmul(X[0][32 * head:32 * head + 32, c * S + P:(c + 1) * S],
                                                va[:, par, 1, first_head + head, :], pk1[:, p, c, head, :],
                                                start=False, stop=True)
                    last.then_inc(pv_ps, 1)

                def transpose_rows(i):
                    pe.wait_ge(xf_ready, i - 2)
                    for t in range(RT):
                        last = nc.tensor.transpose(X[3][:, t * P:(t + 1) * P], rows_and_slots(i)[0][:, t, 0, 0:D], ident)
                    last.then_inc(xfT_ps, 2)

                def router(i):
                    pe.wait_ge(xfT_ready, i - 2)
                    for t in range(RT):
                        last = nc.tensor.matmul(X[3][:, t * E:(t + 1) * E], xfT[:, t * P:(t + 1) * P], wg[:, :],
                                                start=True, stop=True)
                    last.then_inc(lg_done, 2)

                def count_rows(i):
                    pe.wait_ge(picked, 12 * (i - 5) + 24)
                    for t in range(RT + 1):
                        for earlier in range(t):
                            last = nc.tensor.matmul(X[3][:, t * E:(t + 1) * E], ones, chosen[:, earlier, :],
                                                    start=earlier == 0, stop=t == RT and earlier == RT - 1)
                        if t < RT:
                            last = nc.tensor.matmul(X[3][:, t * E:(t + 1) * E], before, chosen[:, t, :], start=t == 0, stop=True)
                    last.then_inc(place_ps, 2)

                def values(i, par, even):
                    if not within(i + 1):
                        return
                    pe.wait_ge(xnT_ready, cap(i + 3, NB))
                    wait(pe, x1_ready, i - 1)
                    if sends_at(i, even):
                        pe.wait_ge(place_taken, i - 3)
                    for t in range(NT):
                        last = nc.tensor.matmul(X[3][:, S + t * D:S + (t + 1) * D], xnT[:, 1 - par, t * P:(t + 1) * P], wv[:, :],
                                                start=True, stop=True)
                    last.then_inc(v_ps, 1)

                def iteration(i, h, even):
                    par = 0 if even else 1
                    n_p, p_p, g_p = pair_of(i, h)
                    par_p = 1 - par if h == 0 else par
                    g_e, g_m = 2 * i + h, 2 * i + 2 + h
                    if within(i - 1 + h):
                        weigh_values(g_e - 1, 1 - h, par if h else 1 - par, 1)
                    if within(i + 1):
                        scores_for_max(g_m, h, 0)
                    if within(i + h):
                        pe.wait_ge(split_done, g_e + 2)
                        wait(pe, stack_q, cap(g_p, HALVES))
                        for t in range(NT):
                            last = nc.tensor.transpose(X[2][0:4 * NG, t * P:(t + 1) * P],
                                                       parts[:, t, :, :, :].rearrange("p g a c -> p (g a c)").bitcast(fp32), ident)
                        last.then_inc(maxT_ps, 1)
                    if within(n_p):
                        wait(pe, stack_k, g_p)
                        wait(pe, on_ready, cap(2 * i - 2 + h, 2 * NB))
                        pe.wait_ge(xnT_ready, n_p + 1)
                        project(0, par_p, p_p)
                    if within(i):
                        scores_for_exp(i, g_e, h, par, 0)
                    if h == 0 and within(i - 2):
                        pe.wait_ge(on_ready, 2 * i - 2)
                        pe.wait_ge(v_ready, cap(i + 1, NB))
                        if sends_at(i, even):
                            pe.wait_ge(lg_taken, i - 3)
                        if picks_at(i, even) and (not isinstance(i, int) or i >= 6):
                            pe.wait_ge(place_taken, i - 4)
                        for t in range(NT):
                            last = nc.tensor.transpose(X[3][:, t * P:(t + 1) * P],
                                                       on[:, t, :, :].rearrange("p h d -> p (h d)"), ident)
                        last.then_inc(onT_ps, 1)
                    if h == 1 and sends_at(i, even):
                        pe.wait_ge(xnT_ready, cap(i + 3, NB))
                        pe.wait_ge(x1_ready, cap(i - 1, NB))
                        count_rows(i)
                    if h == 1 and even:
                        values(i, par, even)
                    if within(i + 1):
                        scores_for_max(g_m, h, 1)
                    if within(n_p):
                        wait(pe, maxT_ready, 2 * i + 2 + h)
                        project(1, par_p, p_p)
                    if within(i):
                        scores_for_exp(i, g_e, h, par, 1)
                    if h == 0 and within(i - 2):
                        pe.wait_ge(onT_ready, i - 1)
                        for t in range(NT):
                            last = nc.tensor.matmul(X[3][:, S + t * D:S + (t + 1) * D], onT[:, t * P:(t + 1) * P], wo[:, :],
                                                    start=True, stop=True)
                        last.then_inc(y_ps, 1)
                    if h == 1 and not even:
                        values(i, par, even)
                    if within(i + 1):
                        scores_for_max(g_m, h, 2)
                    if within(i):
                        scores_for_exp(i, g_e, h, par, 2)
                        pe.wait_ge(v_ready, i + 1)
                        weigh_values(g_e, h, par, 0)
                    if h == 1 and picks_at(i, even):
                        pe.wait_ge(xnT_ready, cap(i + 3, NB))
                        pe.wait_ge(v_ready, cap(i + 2, NB))
                        pe.wait_ge(x1_ready, cap(i - 1, NB))
                        transpose_rows(i)
                    if within(i - 1):
                        pe.wait_ge(oT_ready, 2 * i)
                        wait(pe, stack_k, cap(g_p + 1, HALVES))
                        wait(pe, on_ready, 2 * i - 2 + h)
                        for c in range(NC):
                            last = nc.tensor.transpose(X[1][:, c * P:(c + 1) * P], oT[:, 1 - par, c, h * P:(h + 1) * P], ident)
                        last.then_inc(oq_ps, 1)
                    if h == 0 and within(i + 2):
                        pe.wait_ge(xn_ready, i + 3)
                        wait(pe, x1_ready, i - 1)
                        for t in range(NT):
                            last = nc.tensor.transpose(X[3][:, t * P:(t + 1) * P], xn[:, t, :], ident)
                        last.then_inc(xnT_ps, 1)
                    if h == 1 and picks_at(i, even):
                        router(i)
                schedule(pe, iteration)

        with ExitStack() as part_b:
            def sbb(name, shape, dt):
                return part_b.enter_context(nc.sbuf_tensor(name, shape, dt))

            def psb(name, shape, dt=fp32):
                return part_b.enter_context(nc.psum_tensor(name, shape, dt))

            b2 = sbb("b2", [P, E * D], fp32)
            w2 = sbb("w2", [P, E * FC * D], fp32)
            w1_now = sbb("w1_now", [P, 2, 2, 2, F], fp32r)
            bias_now = sbb("bias_now", [P, 2, 2 * FC], fp32)
            t64 = [sbb(f"t64_{i}", [P, TILES], fp32) for i in range(3)]
            weight = sbb("weight", [P, 2, TILES], fp32)
            xg = sbb("xg", [P, 2, 4, ROW], fp32)
            result_next = sbb("result_next", [P, 2, 4], u32)
            result_now = sbb("result_now", [P, 2, 4], u32)
            xhl = sbb("xhl", [P, 2, 2, CHUNK], fp32r)
            sa = sbb("sa", [P, 2, CHUNK], fp32)
            hT = sbb("hT", [P, 2, FC, CHUNK], fp32)
            ys = sbb("ys", [P, 2, 4, D], fp32)
            yg = sbb("yg", [P, 4, 2, QT, D], fp32)

            ab_ps = [[psb(f"ab_ps{i}{j}", [P, CHUNK]) for j in range(2)] for i in range(2)]
            y_psb = [psb(f"y_psb{i}", [P, 512]) for i in range(2)]
            xt_ps = psb("xt_ps", [P, CHUNK])
            w_split = sem("w_split")
            w_hi = sem("w_hi")
            exp_wanted = sem("exp_wanted")
            exp_done = sem("exp_done")
            w2_loaded = sem("w2_loaded")
            xg_loaded = [sem(f"xg_loaded{i}") for i in range(2)]
            xgT_ps = sem("xgT_ps")
            xhi_ready = sem("xhi_ready")
            xhl_ready = sem("xhl_ready")
            ab_done = sem("ab_done")
            bias_ready = sem("bias_ready")
            next_taken = sem("next_taken")
            next_moved = sem("next_moved")
            silu_ready = sem("silu_ready")
            h_ready = sem("h_ready")
            y_done = sem("y_done")
            y_ready = sem("y_ready")
            y_scattered = [sem(f"y_scattered{i}") for i in range(2)]
            y_loaded = [sem(f"y_loaded{i}") for i in range(4)]
            mixed = sem("mixed")
            out_stored = sem("out_stored")
            turn = sem("turn")
            half_mixed = sem("half_mixed")
            second_weighted = sem("second_weighted")

            def experts(eng, first, n):
                return nc.values_load_multi_w_load_instructions(expert[0:1, bass.ds(first + 1, n)], [eng.engine],
                                                                min_val=0, max_val=E - 1)[1]

            def slot_schedule(eng, iteration, load=True):
                def step(j):
                    e = experts(eng, max(j - 1, -1), 3) if load else None
                    if load and j < 0:
                        e = (None,) + e
                    iteration(j // 2, j % 2, e, nxt=j + 1 < SLOT_TILES, mid=0 <= j < SLOT_TILES, last=j >= 1)
                for j in range(-1, 2):
                    step(j)
                with eng.Fori(1, SLOT_TILES // 2, 1) as k:
                    e = experts(eng, 2 * k - 1, 4) if load else (0,) * 4
                    for s in range(2):
                        iteration(k, s, e[s:s + 3], nxt=True, mid=True, last=True)
                for j in range(SLOT_TILES - 1, SLOT_TILES + 1):
                    step(j)

            block_b = part_b.enter_context(nc.Block())

            @block_b.sync
            def _(sp):
                def tiles_of(first_tile, n):
                    return nc.values_load_multi_w_load_instructions(slot_tile[0:1, bass.ds(first_tile + 1, n)], [sp.engine],
                                                                    min_val=0, max_val=E * REGION + EMPTY_TILES - 1)[1]

                def load(k, s, tile=None):
                    j = 2 * k + s
                    wait(sp, xgT_ps, j - 1)
                    wait(sp, next_taken, j - 1)
                    tile = tiles_of(j, 1)[0] if tile is None else tile
                    rows = xs_dram[bass.ds(tile * CHUNK, CHUNK), :].rearrange("(t p) r -> p t r", p=P)
                    sp.dma_start(xg[:, s, :, :], rows).then_inc(xg_loaded[s], 16)
                first_tiles = tiles_of(0, 2)
                sp.wait_ge(tails_filled, 16 * E)
                sp.wait_ge(empty_filled, 16)
                sp.wait_ge(scattered, 16 * 2 * TILES)
                load(0, 0, first_tiles[0])
                load(0, 1, first_tiles[1])
                sp.dma_start(w2[:, :], w2_in).then_inc(w2_loaded, 16)
                sp.dma_start(b2[:, :], b2_in.rearrange("(a e) d -> a (e d)", a=1)
                             .to_broadcast([P, E * D])).then_inc(w2_loaded, 16)
                with sp.Fori(1, SLOT_TILES // 2, 1) as k:
                    load(k, 0)
                    load(k, 1)
                load(SLOT_TILES // 2, 0)

                sp.wait_ge(y_scattered[0], 64 * ((SLOT_TILES + 1) // 2))
                sp.wait_ge(y_scattered[1], 64 * (SLOT_TILES // 2))

                def load_results(q, m):
                    for choice in range(2):
                        rows = ys_dram[bass.ds(choice * TILES * P + q * CHUNK, CHUNK), :].rearrange("(t p) d -> p t d", p=P)
                        sp.dma_start(yg[:, m, choice, :, :], rows).then_inc(y_loaded[m], 16)

                def store(q):
                    sp.wait_ge(mixed, q + 1)
                    sp.dma_start(out_rows[:, bass.ds(QT * q, QT), :], xs[:, bass.ds(QT * q, QT), :]).then_inc(out_stored, 16)
                out_rows = out.rearrange("b (t p) d -> p (b t) d", p=P)
                for m in range(4):
                    load_results(m, m)
                with sp.Fori(0, QUADS // 4 - 1, 1) as k:
                    for m in range(4):
                        store(4 * k + m)
                        load_results(4 * k + 4 + m, m)
                for m in range(4):
                    store(QUADS - 4 + m)
                sp.wait_ge(out_stored, 16 * QUADS)

            @block_b.gpsimd
            def _(pool):
                def iteration(k, s, e, nxt, mid, last):
                    if last:
                        pool.wait_ge(y_ready, 2 * k + s)
                        pool.sem_inc(turn, 1)
                        for t in range(4):
                            nc.gpsimd.indirect_dma_start(
                                ys_dram, bass.IndirectOffsetOnAxis(result_now[:, 1 - s, t:t + 1], 0),
                                ys[:, 1 - s, t, :], None).then_inc(y_scattered[1 - s], 16)
                slot_schedule(pool, iteration, load=False)

            @block_b.scalar
            def _(act):
                act.wait_ge(exp_wanted, 1)
                nc.scalar.activation(t64[1][:, :], t64[0][:, :], ACT.Exp).then_inc(exp_done, 1)
                act.wait_ge(routed, 1)
                act.wait_ge(experts_loaded, 48)

                def iteration(k, s, e, nxt, mid, last):
                    j = 2 * k + s

                    def weights():
                        nc.scalar.activation(w1_now[:, 1 - s, 0, :, :].rearrange("p a f -> p (a f)"),
                                             w1[:, bass.ds(e[2], 1), :, :].rearrange("p e a f -> p (e a f)"),
                                             ACT.Identity, bias=0.0, scale=ln_w[:, 0:1]).then_inc(w_hi, 1)
                    if not mid and nxt:
                        weights()
                    if mid:
                        act.wait_ge(bias_ready, j + 1)
                    for c in range(FC):
                        if mid:
                            act.wait_ge(ab_done, 8 * j + 2 * c + 1)
                            nc.scalar.activation(sa[:, c % 2, :], ab_ps[c % 2][0][:, :], ACT.Silu,
                                                 bias=bias_now[:, s, c:c + 1]).then_inc(silu_ready, 1)
                        if nxt and c == 0:
                            act.wait_ge(xgT_ps, j + 2)
                            wait(act, ab_done, 8 * j)
                            nc.scalar.copy(xhl[:, 1 - s, 0, :], xt_ps[:, :]).then_inc(xhi_ready, 1)
                        if nxt and mid and c == 1:
                            weights()
                slot_schedule(act, iteration)
                with act.Fori(0, QUADS // 4, 1) as k:
                    for m in range(4):
                        act.wait_ge(y_loaded[m], 32 * (k + 1))
                        for t in range(QT):
                            last = nc.scalar.activation(yg[:, m, 1, t, :], yg[:, m, 1, t, :], ACT.Identity, bias=0.0,
                                                        scale=weight[:, 1, bass.ds(QT * (4 * k + m) + t, 1)])
                        last.then_inc(second_weighted, 1)

            @block_b.vector
            def _(dve):
                links = [0]

                def link(instruction):
                    links[0] += 1
                    instruction.then_inc(mix_chain, 1)
                    dve.wait_ge(mix_chain, links[0])

                tt, ts_, stt = nc.vector.tensor_tensor, nc.vector.tensor_scalar, nc.vector.scalar_tensor_tensor
                tt(t64[0][:, :], best[:, 1, :], best[:, 0, :], ALU.subtract).then_inc(exp_wanted, 1)
                dve.wait_ge(exp_done, 1)
                link(ts_(t64[2][:, :], t64[1][:, :], 1.0, None, ALU.add))
                link(nc.vector.reciprocal(weight[:, 0, :], t64[2][:, :]))
                link(tt(weight[:, 1, :], weight[:, 0, :], t64[1][:, :], ALU.mult))
                dve.wait_ge(routed, 1)
                dve.wait_ge(experts_loaded, 48)

                def iteration(k, s, e, nxt, mid, last):
                    j, o = 2 * k + s, 1 - s

                    def hidden(c):
                        dve.wait_ge(silu_ready, 4 * j + c + 1)
                        dve.wait_ge(ab_done, 8 * j + 2 * c + 2)
                        stt(hT[:, s, c, :], ab_ps[c % 2][1][:, :], bias_now[:, s, FC + c:FC + c + 1], sa[:, c % 2, :],
                            ALU.add, ALU.mult).then_inc(h_ready, 1)
                    if mid:
                        wait(dve, y_done, j - 1)
                        hidden(0)
                    if last:
                        dve.wait_ge(next_taken, j)
                        wait(dve, y_scattered[o], 64 * (k if s else k - 1))
                        nc.vector.tensor_copy(result_now[:, o, :], result_next[:, o, :]).then_inc(next_moved, 1)
                    if nxt:
                        dve.wait_ge(xhi_ready, j + 2)
                        tt(xhl[:, o, 1, :], xt_ps[:, :], xhl[:, o, 0, :].bitcast(fp32), ALU.subtract).then_inc(xhl_ready, 1)
                        if last:
                            dve.wait_ge(next_moved, j)
                        nc.vector.tensor_copy(result_next[:, o, :], xg[:, o, :, D].bitcast(u32)).then_inc(next_taken, 1)
                        nc.vector.tensor_copy(bias_now[:, o, :], b1[:, bass.ds(e[2], 1), :]
                                              .rearrange("p a c -> p (a c)")).then_inc(bias_ready, 1)
                    if mid:
                        hidden(1)
                    if nxt:
                        dve.wait_ge(w_hi, j + 2)
                        stt(w1_now[:, o, 1, :, :], w1[:, bass.ds(e[2], 1), :, :].rearrange("p e a f -> p (e a) f"), ln_w[:, 0:1],
                            w1_now[:, o, 0, :, :].bitcast(fp32), ALU.mult, ALU.subtract).then_inc(w_split, 1)
                    if last:
                        if isinstance(k, int) and j == 1:
                            dve.wait_ge(w2_loaded, 32)
                        dve.wait_ge(y_done, j)
                        tt(ys[:, o, :, :], y_psb[o][:, :].rearrange("p (t d) -> p t d", d=D),
                           b2[:, bass.ds(e[0] * D, D)].unsqueeze(1).to_broadcast([P, 4, D]), ALU.add).then_inc(y_ready, 1)
                    if mid:
                        hidden(2)
                        hidden(3)
                slot_schedule(dve, iteration)

                def mix(k, m):
                    q = 4 * k + m
                    dve.wait_ge(y_loaded[m], 32 * (k + 1))
                    for t in range(QT):
                        tile = bass.ds(QT * q + t, 1)
                        last = stt(yg[:, m, 0, t, :], yg[:, m, 0, t, :], weight[:, 0, tile],
                                   xs[:, tile, :].rearrange("p a d -> p (a d)"), ALU.mult, ALU.add)
                    last.then_inc(half_mixed, 1)
                    dve.wait_ge(half_mixed, q + 1)
                    dve.wait_ge(second_weighted, q + 1)
                    tt(xs[:, bass.ds(QT * q, QT), :], yg[:, m, 0, :, :], yg[:, m, 1, :, :], ALU.add).then_inc(mixed, 1)
                with dve.Fori(0, QUADS // 4, 1) as k:
                    for m in range(4):
                        mix(k, m)

            @block_b.tensor
            def _(pe):
                pe.wait_ge(routed, 1)

                def iteration(k, s, e, nxt, mid, last):
                    j, o = 2 * k + s, 1 - s

                    def hidden(c):
                        wait(pe, h_ready, 4 * j + c - 1)
                        for ab in range(2):
                            for m, (xpart, wpart) in enumerate(((0, 0), (0, 1), (1, 0))):
                                last_i = nc.tensor.matmul(ab_ps[c % 2][ab][:, :], w1_now[:, s, wpart, ab, c * P:(c + 1) * P],
                                                          xhl[:, s, xpart, :], start=m == 0, stop=m == 2)
                            last_i.then_inc(ab_done, 1)
                    if mid:
                        pe.wait_ge(w_split, j + 1)
                        pe.wait_ge(xhl_ready, j + 1)
                        hidden(0)
                    if nxt:
                        pe.wait_ge(xg_loaded[o], 16 * (k + 1 + s))
                        for t in range(4):
                            last_i = nc.tensor.transpose(xt_ps[:, t * P:(t + 1) * P], xg[:, o, t, 0:D], ident)
                        last_i.then_inc(xgT_ps, 1)
                    if mid:
                        hidden(1)
                    if last:
                        if isinstance(k, int) and j == 1:
                            pe.wait_ge(w2_loaded, 32)
                        pe.wait_ge(h_ready, 4 * j)
                        wait(pe, y_ready, j - 2)
                        for t in range(4):
                            for c in range(FC):
                                last_i = nc.tensor.matmul(y_psb[o][:, t * D:(t + 1) * D], hT[:, o, c, t * P:(t + 1) * P],
                                                          w2[:, bass.ds(e[0] * F + c * D, D)], start=c == 0, stop=c == FC - 1)
                        last_i.then_inc(y_done, 1)
                    if mid:
                        hidden(2)
                        hidden(3)
                slot_schedule(pe, iteration)


def bf16_parts(value, np, bf16):
    high = float(np.float32(value).astype(bf16))
    return high, value - high


def layout_constants():
    import math
    import numpy as np
    bf16 = np.dtype("bfloat16")
    P, S, NC, NG, H, E, TILES = 128, 256, 4, 4, 16, 8, 64
    row = np.arange(P) % 32
    f32 = np.zeros((P, 3 + P), np.float32)
    f32[:, 0] = -0.5
    f32[:, 1] = np.where((row >= 20) & (row < 28), -1, 0)
    f32[:, 2] = np.where((row >= 12) & (row < 20), -1, 0)
    f32[:, 3:] = np.eye(P)
    q = np.arange(P)
    causal = np.where(q[None, :] <= q[:, None], 0, -1e30)
    pos = np.zeros((P, S))
    pos[0] = np.arange(S)
    pos[1:3] = 1
    const_q, const_k = np.zeros((2, P, NC, P))
    h = np.arange(1, H + 1, dtype=np.float32)
    slopes = (np.float32(1) / np.power(np.float32(256), h / np.float32(H))).astype(np.float32)
    for c in range(NC):
        for g in range(NG):
            slope = float(slopes[NG * c + g])
            m, e = math.frexp(slope)
            high = math.ldexp(round(m * 4096), e - 12)
            for base, part in ((0, high), (2, slope - high)):
                p0, p1 = bf16_parts(part, np, bf16)
                const_q[1, c, 32 * g + base], const_q[2, c, 32 * g + base] = p0, p1
                const_q[0, c, 32 * g + base + 1] = -1
                const_k[0, c, 32 * g + base] = 1
                const_k[1, c, 32 * g + base + 1], const_k[2, c, 32 * g + base + 1] = p0, p1
            const_k[1, c, 32 * g + 28] = const_k[1, c, 32 * g + 29] = 1
    b16 = np.concatenate([np.eye(P), np.tile(causal, (1, 4)), np.tile(causal.T, (1, 4)), pos,
                          const_q.reshape(P, -1), const_k.reshape(P, -1)], 1).astype(bf16)
    route = np.concatenate([np.tile(E - np.arange(E), (P, 1)), np.tile(17 * 512 * np.arange(E), (P, 1)),
                            np.tile(np.arange(2 * TILES // 4 + E + 2) - 1.0, (P, 1))],
                           1).astype(np.float32)
    route16 = np.concatenate([q[:, None] < q[None, :], np.ones((P, P))], 1).astype(bf16)
    empty = np.zeros((15 * 512, P + 4), np.uint32)
    empty[:, P] = 2 * TILES * P + np.arange(15 * 512)
    result_rows = (np.arange(2)[None, None, :] * TILES * P + np.arange(TILES)[None, :, None] * P
                   + q[:, None, None]).astype(np.uint32)
    return f32, b16, route, route16, empty.view(np.float32), result_rows


def wide(w, np):
    out = np.zeros((128, 4, 4, 32), w.dtype)
    wt = w.T.reshape(128, 4, 4, 8)
    for copy in range(3):
        out[:, :, :, 4 + 8 * copy:12 + 8 * copy] = wt
    return out.reshape(128, 4, 128)


def kernel(L0_attn_x, L0_attn_W_Q, L0_attn_W_K, L0_attn_W_V, L0_attn_W_O, L0_ffn_ln_w, L0_ffn_Wg, L0_ffn_bg, L0_ffn_W1a,
           L0_ffn_b1a, L0_ffn_W1b, L0_ffn_b1b, L0_ffn_W2, L0_ffn_b2):
    import numpy as np
    import concourse.bacc as bacc
    from concourse.bass_utils import run_bass_kernel_spmd

    f32, b16, route, route16, empty, result_rows = layout_constants()
    E, F, D = L0_ffn_W2.shape
    w2 = np.asarray(L0_ffn_W2).reshape(E, F // 128, 128, D).transpose(2, 0, 1, 3).reshape(128, E * F // 128 * D)
    b1 = np.stack([np.asarray(b).reshape(E, F // 128, 128) for b in (L0_ffn_b1a, L0_ffn_b1b)], 1)
    b1 = b1.transpose(3, 0, 1, 2).reshape(128, E, 2 * F // 128)
    ins = [L0_attn_x, wide(np.asarray(L0_attn_W_Q), np), wide(np.asarray(L0_attn_W_K), np), np.asarray(L0_attn_W_V).T,
           np.asarray(L0_attn_W_O).T, f32, b16, L0_ffn_ln_w, L0_ffn_Wg, L0_ffn_bg, L0_ffn_W1a, b1, L0_ffn_W1b, w2,
           L0_ffn_b2, route, route16, empty, result_rows]
    nc = bacc.Bacc("TRN2", target_bir_lowering=False, num_devices=1)
    arrays, args = {}, []
    for n, a in enumerate(ins):
        a = np.ascontiguousarray(a)
        arrays[f"in_{n}_dram"] = a
        args.append(nc.dram_tensor(f"in_{n}_dram", a.shape, mybir.dt.from_np(a.dtype), kind="ExternalInput").ap())
    args.append(nc.dram_tensor("out_0_dram", L0_attn_x.shape, mybir.dt.float32, kind="ExternalOutput").ap())
    build_program(nc, *args)
    r = run_bass_kernel_spmd(nc, [arrays], core_ids=[0])
    return r.results[0]["out_0_dram"]
```
